# Optimizing a Trainium2 kernel written in Bass

```python
import numpy as np
import jax
import jax.numpy as jnp

def _softmax(x, axis=-1):
    return jax.nn.softmax(x, axis=axis)

def _gelu(x):
    return jax.nn.gelu(x, approximate=True)

def _silu(x):
    return jax.nn.silu(x)

def _sigmoid(x):
    return jax.nn.sigmoid(x)

def _layernorm(x, axis=-1, eps=1e-05):
    m = jnp.mean(x, axis=axis, keepdims=True)
    v = jnp.var(x, axis=axis, keepdims=True)
    return (x - m) / jnp.sqrt(v + eps)

def _scatter_add(tgt, idx, src, axis=0):
    return tgt.at[idx].add(src)

def _segment_sum(src, seg, n):
    return jax.ops.segment_sum(src, seg, n)
kernel_name = 'mk_audio_tower_d1_tok_audfeat256_r4_e2315c'

def setup_inputs(seed: int=0):
    np.random.seed(seed)
    _w = jnp.asarray

    def _rec_inputs():
        import jax
        import jax.numpy as jnp
        _rk = jax.random.key(seed)
        x = -0.000154596 + 0.999967 * jax.random.normal(jax.random.fold_in(_rk, 1), (32, 375, 64), jnp.float32)
        return x
    x = _rec_inputs()

    def _L0_tok_setup():
        import jax, jax.numpy as jnp
        import numpy as np
        RATIO = 0.5
        key = jax.random.key(seed)
        k1, k2 = jax.random.split(key)
        B, N, F = (32, 4096, 64)
        inputs = jax.random.normal(k1, (B, N, F), dtype=jnp.float32)
        score_proj = jax.random.normal(k2, (F, 1), dtype=jnp.float32) * (1.0 / np.sqrt(F))
        return {'inputs': inputs, 'score_proj': score_proj}
    _L0_tok_all = _L0_tok_setup()
    _L0_tok_in = {k: v for k, v in _L0_tok_all.items() if k in ('score_proj',)}
    del _L0_tok_all

    def _L0_attn_setup():
        import jax, jax.numpy as jnp
        import numpy as np
        import math
        B, L, C = (1024, 64, 64)
        H = 8
        META_H = 96

        def _rel_coords_log(W):
            c0 = jnp.zeros((W,), jnp.float32)
            c1 = jnp.arange(W, dtype=jnp.float32)
            coords = jnp.stack([c0, c1], axis=0)
            rel = coords[:, :, None] - coords[:, None, :]
            rel = rel.transpose(1, 2, 0).reshape(-1, 2)
            return jnp.sign(rel) * jnp.log1p(jnp.abs(rel))
        key = jax.random.key(seed)
        ks = jax.random.split(key, 8)
        s = 0.02
        return {'x': jax.random.normal(ks[0], (B, L, C), jnp.float32), 'qkv_w': jax.random.normal(ks[1], (3 * C, C), jnp.float32) * s, 'qkv_b': jnp.zeros((3 * C,), jnp.float32), 'proj_w': jax.random.normal(ks[2], (C, C), jnp.float32) * s, 'proj_b': jnp.zeros((C,), jnp.float32), 'logit_scale': jnp.full((H,), math.log(10.0), jnp.float32), 'mlp1_w': jax.random.normal(ks[3], (META_H, 2), jnp.float32) * s, 'mlp1_b': jnp.zeros((META_H,), jnp.float32), 'mlp2_w': jax.random.normal(ks[4], (H, META_H), jnp.float32) * s, 'mlp2_b': jnp.zeros((H,), jnp.float32)}
    _L0_attn_all = _L0_attn_setup()
    _L0_attn_in = {k: v for k, v in _L0_attn_all.items() if k in ('qkv_w', 'qkv_b', 'proj_w', 'proj_b', 'logit_scale', 'mlp1_w', 'mlp1_b', 'mlp2_w', 'mlp2_b')}
    del _L0_attn_all

    def _L0_ffn_setup():
        import jax, jax.numpy as jnp
        import numpy as np
        E = 8
        K = 2
        D = 64
        H = 128
        DOUT = 64
        EPS = 1e-05
        key = jax.random.key(seed)
        ks = jax.random.split(key, 9)
        s = 0.02
        return {'x': jax.random.normal(ks[0], (4, 2048, D), jnp.float32), 'gamma': 1.0 + 0.05 * jax.random.normal(ks[1], (D,), jnp.float32), 'beta': 0.05 * jax.random.normal(ks[2], (D,), jnp.float32), 'Wr': 0.01 * jax.random.normal(ks[3], (D, E), jnp.float32), 'br': jnp.zeros((E,), jnp.float32), 'W1': s * jax.random.normal(ks[4], (E, D, H), jnp.float32), 'b1': s * jax.random.normal(ks[5], (E, H), jnp.float32), 'W2': s * jax.random.normal(ks[6], (E, H, DOUT), jnp.float32), 'b2': s * jax.random.normal(ks[7], (E, DOUT), jnp.float32)}
    _L0_ffn_all = _L0_ffn_setup()
    _L0_ffn_in = {k: v for k, v in _L0_ffn_all.items() if k in ('gamma', 'beta', 'Wr', 'br', 'W1', 'b1', 'W2', 'b2')}
    del _L0_ffn_all
    return {'x': x, 'L0_tok_score_proj': _L0_tok_in['score_proj'], 'L0_attn_qkv_w': _L0_attn_in['qkv_w'], 'L0_attn_qkv_b': _L0_attn_in['qkv_b'], 'L0_attn_proj_w': _L0_attn_in['proj_w'], 'L0_attn_proj_b': _L0_attn_in['proj_b'], 'L0_attn_logit_scale': _L0_attn_in['logit_scale'], 'L0_attn_mlp1_w': _L0_attn_in['mlp1_w'], 'L0_attn_mlp1_b': _L0_attn_in['mlp1_b'], 'L0_attn_mlp2_w': _L0_attn_in['mlp2_w'], 'L0_attn_mlp2_b': _L0_attn_in['mlp2_b'], 'L0_ffn_gamma': _L0_ffn_in['gamma'], 'L0_ffn_beta': _L0_ffn_in['beta'], 'L0_ffn_Wr': _L0_ffn_in['Wr'], 'L0_ffn_br': _L0_ffn_in['br'], 'L0_ffn_W1': _L0_ffn_in['W1'], 'L0_ffn_b1': _L0_ffn_in['b1'], 'L0_ffn_W2': _L0_ffn_in['W2'], 'L0_ffn_b2': _L0_ffn_in['b2']}

def reference(x, L0_tok_score_proj, L0_attn_qkv_w, L0_attn_qkv_b, L0_attn_proj_w, L0_attn_proj_b, L0_attn_logit_scale, L0_attn_mlp1_w, L0_attn_mlp1_b, L0_attn_mlp2_w, L0_attn_mlp2_b, L0_ffn_gamma, L0_ffn_beta, L0_ffn_Wr, L0_ffn_br, L0_ffn_W1, L0_ffn_b1, L0_ffn_W2, L0_ffn_b2):
    import jax
    import jax.numpy as jnp

    def _L0_tok_ref(inputs, score_proj):
        import jax, jax.numpy as jnp
        import numpy as np
        RATIO = 0.5
        N = inputs.shape[1]
        k = max(int(N * RATIO), 1)
        scores = jnp.einsum('bnf,fo->bn', inputs, score_proj)
        _, top_idx = jax.lax.top_k(scores, k)
        sel_feat = jnp.take_along_axis(inputs, top_idx[:, :, None], axis=1)
        sel_scores = jnp.take_along_axis(scores, top_idx, axis=1)
        gate = jax.nn.sigmoid(sel_scores)[:, :, None]
        return sel_feat * gate

    def _L0_attn_ref(x, qkv_w, qkv_b, proj_w, proj_b, logit_scale, mlp1_w, mlp1_b, mlp2_w, mlp2_b):
        import jax, jax.numpy as jnp
        import numpy as np
        import math
        B, L, C = (1024, 64, 64)
        H = 8
        META_H = 96

        def _rel_coords_log(W):
            c0 = jnp.zeros((W,), jnp.float32)
            c1 = jnp.arange(W, dtype=jnp.float32)
            coords = jnp.stack([c0, c1], axis=0)
            rel = coords[:, :, None] - coords[:, None, :]
            rel = rel.transpose(1, 2, 0).reshape(-1, 2)
            return jnp.sign(rel) * jnp.log1p(jnp.abs(rel))
        b, l, c = x.shape
        h = H
        d = c // h
        qkv = x @ qkv_w.T + qkv_b
        qkv = qkv.reshape(b, l, 3, h, d).transpose(2, 0, 3, 1, 4)
        q, k, v = (qkv[0], qkv[1], qkv[2])
        qn = q / jnp.maximum(jnp.linalg.norm(q, axis=-1, keepdims=True), 1e-12)
        kn = k / jnp.maximum(jnp.linalg.norm(k, axis=-1, keepdims=True), 1e-12)
        attn = jnp.einsum('bhld,bhmd->bhlm', qn, kn)
        scale = jnp.exp(jnp.minimum(logit_scale, math.log(1.0 / 0.01)))
        attn = attn * scale.reshape(1, h, 1, 1)
        rel = _rel_coords_log(l)
        hid = jax.nn.relu(rel @ mlp1_w.T + mlp1_b)
        bias = (hid @ mlp2_w.T + mlp2_b).T.reshape(h, l, l)
        attn = jax.nn.softmax(attn + bias[None], axis=-1)
        out = jnp.einsum('bhlm,bhmd->bhld', attn, v)
        out = out.transpose(0, 2, 1, 3).reshape(b, l, c)
        return out @ proj_w.T + proj_b

    def _L0_ffn_ref(x, gamma, beta, Wr, br, W1, b1, W2, b2):
        import jax, jax.numpy as jnp
        import numpy as np
        E = 8
        K = 2
        D = 64
        H = 128
        DOUT = 64
        EPS = 1e-05
        mu = jnp.mean(x, axis=-1, keepdims=True)
        var = jnp.mean(jnp.square(x - mu), axis=-1, keepdims=True)
        xn = (x - mu) * jax.lax.rsqrt(var + EPS) * gamma + beta
        logits = jnp.einsum('bsd,de->bse', xn, Wr) + br
        top_vals, top_idx = jax.lax.top_k(logits, K)
        w = jax.nn.softmax(top_vals, axis=-1)
        w_full = jnp.einsum('bsk,bske->bse', w, jax.nn.one_hot(top_idx, E, dtype=w.dtype))
        y = jnp.zeros(x.shape[:-1] + (DOUT,), x.dtype)
        for e in range(E):
            h = jax.nn.gelu(jnp.einsum('bsd,dh->bsh', xn, W1[e]) + b1[e], approximate=False)
            y_e = jnp.einsum('bsh,hd->bsd', h, W2[e]) + b2[e]
            y = y + y_e * w_full[..., e, None]
        return y
    h = _L0_tok_ref(x, L0_tok_score_proj)
    h = h + _L0_attn_ref(_layernorm(h, axis=-1), L0_attn_qkv_w, L0_attn_qkv_b, L0_attn_proj_w, L0_attn_proj_b, L0_attn_logit_scale, L0_attn_mlp1_w, L0_attn_mlp1_b, L0_attn_mlp2_w, L0_attn_mlp2_b)
    h = h + _L0_ffn_ref(_layernorm(h, axis=-1), L0_ffn_gamma, L0_ffn_beta, L0_ffn_Wr, L0_ffn_br, L0_ffn_W1, L0_ffn_b1, L0_ffn_W2, L0_ffn_b2)
    return h

_drawn_inputs = setup_inputs


def setup_inputs(seed=0):
    import zlib

    import numpy as np

    out = dict(_drawn_inputs(seed))
    spreads = {'L0_attn_qkv_b': (0.0, 0.297),
     'L0_attn_proj_b': (0.0, 0.1),
     'L0_attn_logit_scale': (2.3025851249694824, 0.6),
     'L0_attn_mlp1_b': (0.0, 0.8),
     'L0_attn_mlp2_b': (0.0, 0.8),
     'L0_ffn_br': (0.0, 0.1)}
    factors = {'L0_attn_qkv_w': 3.375,
     'L0_attn_mlp1_w': 8.0,
     'L0_attn_mlp2_w': 8.0,
     'L0_ffn_gamma': 8.0,
     'L0_ffn_beta': 8.0,
     'L0_ffn_Wr': 4.323,
     'L0_ffn_W1': 3.077,
     'L0_ffn_b1': 8.0,
     'L0_ffn_W2': 3.025,
     'L0_ffn_b2': 2.935}
    for name, (base, spread) in spreads.items():
        noise = np.random.default_rng([zlib.crc32(name.encode()), seed]).standard_normal(out[name].shape)
        drawn = base * np.exp(spread * noise) if base else spread * noise
        out[name] = jnp.asarray(drawn.astype(out[name].dtype))
    for name, factor in factors.items():
        out[name] = (out[name] * factor).astype(out[name].dtype)
    return out
```

```python
import concourse.bass as bass
from concourse import mybir
from contextlib import ExitStack

B, N, C = 32, 375, 64
NSEL = N // 2
H, D = 8, 8
E, HID = 8, 128
META = 96
HALF = (NSEL + 1) // 2
LQ = 2 * HALF
REST = NSEL - HALF
TP, TC = 125, 3
REL = LQ + NSEL - 1
KSCALE = 16.0
WSCALE = 64.0
QW = 32
NCH, CB = 8, 4
CT = 2 * CB
EPS = 1e-5
MAGIC = float(0x5F3759DF)


class Batch:

    def __init__(self, pair, rest):
        self.pair, self.rest = pair, rest

    def __add__(self, d):
        return Batch(self.pair, self.rest + d)

    @property
    def n(self):
        return 2 * self.pair + self.rest

    @property
    def buf(self):
        return self.rest % 2

    @property
    def turn(self):
        return self.pair + self.rest // 2

    def within(self, count):
        return not isinstance(self.pair, int) or 0 <= self.n < count


def passed(eng, sem, value):
    if not isinstance(value, int) or value > 0:
        eng.wait_ge(sem, value)


def held(eng, sem, value, spare):
    passed(eng, sem, value)
    eng.sem_inc(spare, 1)


def audio_tower(nc, x, score_proj, qkv_w, qkv_b, proj_w, proj_b, logit_scale, mlp1_w, mlp1_b,
                mlp2_w, mlp2_b, gamma, beta, Wr, br, W1, b1, W2, b2, rel_log, out):
    f32, f16, i32 = mybir.dt.float32, mybir.dt.float16, mybir.dt.int32
    ALU, ACT, AX = mybir.AluOpType, mybir.ActivationFunctionType, mybir.AxisListType

    bias_dram = nc.dram_tensor("bias_scratch", (3, H, HALF, REL), f16, kind="Internal").ap()

    ctx = ExitStack()
    with ctx:
        def sb(name, shape, dt=f32):
            return ctx.enter_context(nc.sbuf_tensor(name, shape, dt))

        def ps(name, banks):
            return ctx.enter_context(nc.psum_tensor(name, [128, 512 * banks], f32))

        def sem(name):
            return ctx.enter_context(nc.semaphore(name))

        ident = sb("ident", [128, 128])
        ident16 = sb("ident16", [128, 128], f16)
        before = sb("before", [TP, TC, N])
        tiny = sb("tiny", [TP, N])
        place_i = sb("place_i", [TP, LQ], i32)
        place = sb("place", [TP, LQ])
        wscore = sb("wscore", [TP, C])
        w_qkv = sb("w_qkv", [C + 1, 3 * C])
        w_proj = sb("w_proj", [C + 1, C])
        w_raw = sb("w_raw", [META, 2, C])
        wp_raw = sb("wp_raw", [C, C])
        qk_scale = sb("qk_scale", [HALF, 2, 2, H])
        ls = sb("ls", [HALF, H])
        rel = sb("rel", [2, 2 * REL])
        m1t = sb("m1t", [2, META])
        m1b = sb("m1b", [META, 1])
        m2t = sb("m2t", [META, H])
        m2rep = sb("m2rep", [META, H, 128])
        m2b = sb("m2b", [128, H])
        m2bs = sb("m2bs", [128, H])
        hid = sb("hid", [META, 2 * REL])
        hT = sb("hT", [HID, 2, E, CT * HALF])
        hT_flat = hT[0:HALF, :, :, :].rearrange("p b e n -> p (b e n)")
        dist = hT_flat[:, 0:2 * H * REL].rearrange("p (r h w) -> p r h w", r=2, h=H)
        dist16 = hT_flat[:, 2 * H * REL:2 * H * REL + 3 * H * REL // 2].bitcast(f16).rearrange("p (r h w) -> p r h w", r=3, h=H)
        bias_q = sb("bias_q", [128, 2, H, NSEL], f16)
        bias_k = sb("bias_k", [128, 2, 2, H, LQ], f16)

        X = sb("X", [TP, 2, TC, C + 1])
        prod = sb("prod", [TP, TC, C])
        flags = sb("flags", [TP, TC, N], f16)
        rank = sb("rank", [TP, 2, TC])
        onehot = sb("onehot", [TP, 2, TC, LQ])
        sel = sb("sel", [HALF, 2, C + 1])
        egate = sb("egate", [HALF, 2])
        gate = sb("gate", [HALF, 2])
        stats = sb("stats", [HALF, 2, 6])
        mv = sb("mv", [HALF, 2, 2])
        ln_v = sb("ln_v", [HALF, 2])
        ln_i = sb("ln_i", [HALF, 2], i32)
        ln_y = sb("ln_y", [HALF, 2])
        ln_t = sb("ln_t", [HALF, 2])
        xn = sb("xn", [HALF, 2, C])
        xnT = sb("xnT", [C + 1, LQ])
        qkv = sb("qkv", [HALF, 2, 2, 3 * C])
        sq = sb("sq", [HALF, 2, 2 * C])
        nv = sb("nv", [HALF, 4 * H])
        ni = sb("ni", [HALF, 4 * H], i32)
        ny = sb("ny", [HALF, 4 * H])
        nt = sb("nt", [HALF, 4 * H])
        qn = sb("qn", [HALF, 2, 2 * C])
        stack = sb("stack", [HALF, 2, 2, 2, H, QW], f16)
        qT1 = sb("qT1", [128, 2, LQ], f16)
        kT = sb("kT", [128, 2, 2, 4, LQ], f16)
        qT2 = sb("qT2", [128, 2, LQ], f16)
        V = sb("V", [128, 2, 2, H, QW])
        P = sb("P", [128, 4, 4, LQ])
        oT = sb("oT", [128, 2, LQ])
        rz = sb("rz", [HALF, 16])
        on = sb("on", [HALF, 2, C])
        onT = sb("onT", [C + 1, LQ])
        hsel = sb("hsel", [HALF, B, 2, C])

        w1raw = sb("w1raw", [128, E, HID])
        w1s = sb("w1s", [128, E, 2, HID], f16)
        w2 = sb("w2", [HID, E, C])
        b1c = sb("b1c", [HID, E])
        b1raw = sb("b1raw", [E, HID])
        b2raw = sb("b2raw", [1, E * C])
        b2hl = sb("b2hl", [1, 2, E * C], f16)
        ones16 = sb("ones16", [1, HALF], f16)
        wr_raw = sb("wr_raw", [128, E])
        wrs = sb("wrs", [128, 2, E], f16)
        br_b = sb("br_b", [HALF, E])
        gam = sb("gam", [HALF, C])
        bet = sb("bet", [HALF, C])
        prio_i = sb("prio_i", [HALF, E], i32)
        prio = sb("prio", [HALF, E])
        n_stats = sb("n_stats", [HALF, CT, 6])
        n_mv = sb("n_mv", [HALF, CT, 2])
        n_v = sb("n_v", [HALF, CT])
        n_i = sb("n_i", [HALF, CT], i32)
        n_y = sb("n_y", [HALF, CT])
        n_t = sb("n_t", [HALF, CT])
        n_x = sb("n_x", [HALF, CT, C])
        n_z = sb("n_z", [HALF, CT, C])
        xs = sb("xs", [HALF, CT, 2 * C], f16)
        xsT = sb("xsT", [128, 2, CT * HALF], f16)
        lg = sb("lg", [HALF, CT, E])
        lg2 = sb("lg2", [HALF, CT, E])
        eq = sb("eq", [HALF, CT, E])
        oh1 = sb("oh1", [HALF, CT, E])
        oh2 = sb("oh2", [HALF, CT, E])
        top1 = sb("top1", [HALF, CT])
        top2 = sb("top2", [HALF, CT])
        pick = sb("pick", [HALF, CT])
        dif = sb("dif", [HALF, CT])
        th = sb("th", [HALF, CT])
        wa = sb("wa", [HALF, CT])
        wb = sb("wb", [HALF, CT])
        wfull = sb("wfull", [HALF, 2, CT, E])
        yw = sb("yw", [HALF, 2, E, C])
        yr = sb("yr", [HALF, 2, C])
        yo = sb("yo", [HALF, 2, CT, C])

        s1 = ps("s1", 2)
        s2 = ps("s2", 4)
        MA = ps("MA", 1)
        MB = ps("MB", 1)
        MA16 = MA[:, :].bitcast(f16)

        names = """c_wscore c_qkvw c_qkvb c_projw c_projb c_ls c_rel c_mlp c_moe c_moeb const_pool const_dve const_act
            const_pe bias_stored bias_loaded score ranks_row rank_done onehot_done gathered sel_out
            gate_steps ln_newton xn_done xnT_ready xnT_out qkv_ready qkv_out norm_steps qk_newton
            stack_dve stack_hi stack_pool t1_ready t1_out v_done s1_ready neg_max t2_ready t2_out
            s2_ready exp_done pv_done oT_out to_ready on_done onT_ready onT_out pr_ready h_done
            n_stat n_pool n_hi xsT_ready xsT_out lg_ready gates th_done h_ready gelu_done y_ready
            y_dve out_done0 out_done1""".split()
        S = {n: sem(n) for n in names}
        (c_wscore, c_qkvw, c_qkvb, c_projw, c_projb, c_ls, c_rel, c_mlp, c_moe, c_moeb, const_pool, const_dve, const_act,
         const_pe, bias_stored, bias_loaded, score, ranks_row, rank_done, onehot_done, gathered,
         sel_out, gate_steps, ln_newton, xn_done, xnT_ready, xnT_out, qkv_ready, qkv_out,
         norm_steps, qk_newton, stack_dve, stack_hi, stack_pool, t1_ready, t1_out, v_done,
         s1_ready, neg_max, t2_ready, t2_out, s2_ready, exp_done, pv_done, oT_out, to_ready,
         on_done, onT_ready, onT_out, pr_ready, h_done, n_stat, n_pool, n_hi, xsT_ready, xsT_out,
         lg_ready, gates, th_done, h_ready, gelu_done, y_ready, y_dve, out_done0,
         out_done1) = [S[n] for n in names]
        x_loaded = [sem("x_loaded0"), sem("x_loaded1")]
        spare = sem("spare")
        out_done = [out_done0, out_done1]

        x_v = x.rearrange("b (p c) f -> b p c f", c=TC)

        FIRST, LAST = 2, B - 4

        def steps(eng, step):
            for t in range(-4, FIRST):
                step(Batch(0, t))
            with eng.Fori(FIRST // 2, LAST // 2) as k:
                step(Batch(k, 0))
                step(Batch(k, 1))
            for t in range(LAST, B + 1):
                step(Batch(0, t))

        def chunk_steps(eng, step):
            for c in range(-2, 2):
                step(Batch(0, c))
            with eng.Fori(1, (NCH - 2) // 2) as k:
                step(Batch(k, 0))
                step(Batch(k, 1))
            for c in range(NCH - 2, NCH):
                step(Batch(0, c))

        block = ctx.enter_context(nc.Block())

        @block.sync
        def _(sp):
            def load_x(b):
                passed(sp, gathered, b.n - 1)
                sp.dma_start(X[:, b.buf, :, 0:C], x_v[b.n, :, :, :]).then_inc(x_loaded[b.buf], 16)

            sp.dma_start(wscore[:, :], score_proj.rearrange("f o -> o f").broadcast_to([TP, C])).then_inc(c_wscore, 16)
            load_x(Batch(0, 0))
            load_x(Batch(0, 1))
            for tile in range(2):
                for part in range(2):
                    src = bass.AP(bias_dram.tensor, bias_dram.offset + part * H * HALF * REL + NSEL - 1 - HALF * tile,
                                  [[REL - 1, HALF - tile], [HALF * REL, H], [1, LQ]])
                    if tile == 0 and part == 0:
                        sp.wait_ge(bias_stored, 16)
                    sp.dma_start(bias_k[0:HALF - tile, tile, part, :, :], src).then_inc(bias_loaded, 16)
                src = bass.AP(bias_dram.tensor, bias_dram.offset + 2 * H * HALF * REL + NSEL - HALF * tile,
                              [[REL - 1, HALF], [HALF * REL, H], [1, NSEL]])
                sp.dma_start(bias_q[0:HALF, tile, :, :], src).then_inc(bias_loaded, 16)

            def step(t):
                b = t + 6
                if b.within(B):
                    load_x(b)
            for t in range(-4, FIRST):
                step(Batch(0, t))
            with sp.Fori(FIRST // 2, LAST // 2 - 1) as k:
                step(Batch(k, 0))
                step(Batch(k, 1))
            for t in range(LAST - 2, B + 1):
                step(Batch(0, t))

            def store(c):
                if not c.within(NCH):
                    return
                sp.wait_ge(y_dve, 24 * (c.n + 1))
                for half, rows in ((0, HALF), (1, REST)):
                    dst = out[bass.ds(c.n * CB, CB), half * HALF:half * HALF + rows, :].rearrange("b p f -> p b f")
                    src = yo[0:rows, c.buf, :, :].rearrange("p (b t) f -> p b t f", t=2)[:, :, half, :]
                    sp.dma_start(dst, src).then_inc(out_done[c.buf], 16)

            chunk_steps(sp, store)
            sp.wait_ge(out_done[0], 16 * NCH)
            sp.wait_ge(out_done[1], 16 * NCH)

        @block.gpsimd
        def _(pool):
            nc.gpsimd.memset(ident[:, :], 0.0).then_inc(const_pool, 1)
            nc.gpsimd.memset(tiny[:, :], -1e-37).then_inc(const_pool, 1)
            nc.gpsimd.iota(place_i[:, :], pattern=[[1, LQ]], base=0, channel_multiplier=0).then_inc(const_pool, 1)
            nc.gpsimd.iota(prio_i[:, :], pattern=[[-1, E]], base=E, channel_multiplier=0).then_inc(const_pool, 1)
            pool.wait_ge(const_pool, 4)
            nc.gpsimd.affine_select(out=ident[:, :], in_=ident[:, :], compare_op=ALU.not_equal, fill=1.0,
                                    base=0, pattern=[[-1, 128]], channel_multiplier=1).then_inc(const_pool, 1)
            for c in range(TC):
                nc.gpsimd.affine_select(out=before[:, c, :], in_=tiny[:, :], compare_op=ALU.is_gt, fill=0.0,
                                        base=c, pattern=[[-1, TC], [-3, TP]],
                                        channel_multiplier=TC).then_inc(const_pool, 1)

            def newton(sems, count, base, y, v, t):
                for r in range(3):
                    nc.gpsimd.tensor_tensor(t, y, y, ALU.mult).then_inc(sems, 1)
                    pool.wait_ge(sems, base + 4 * r + 1)
                    nc.gpsimd.tensor_tensor(t, t, v, ALU.mult).then_inc(sems, 1)
                    held(pool, sems, base + 4 * r + 2, spare)
                    nc.gpsimd.tensor_scalar(t, t, -0.5, 1.5, ALU.mult, ALU.add).then_inc(sems, 1)
                    pool.wait_ge(sems, base + 4 * r + 3)
                    nc.gpsimd.tensor_tensor(y, y, t, ALU.mult).then_inc(sems, 1)
                    if r < 2 or count > 12:
                        pool.wait_ge(sems, base + 4 * r + 4)

            def step(t):
                b = t + 2
                if b.within(B):
                    pool.wait_ge(norm_steps, 4 * (b.n + 1))
                    newton(qk_newton, 13, 13 * b.n, ny[:, :], nv[:, :], nt[:, :])
                    passed(pool, stack_dve, 3 * b.n - 2)
                    nc.gpsimd.tensor_tensor(nt[:, :], ny[:, :],
                                            qk_scale[:, :, :, :].rearrange("p t q h -> p (t q h)"),
                                            ALU.mult).then_inc(qk_newton, 1)
                b = t + 1
                if b.within(B):
                    pool.wait_ge(qkv_out, 2 * (b.n + 1))
                    held(pool, pv_done, 4 * (b.n - 1), spare)
                    for tile in range(2):
                        nc.gpsimd.tensor_copy(V[0:HALF, b.buf, tile, :, 0:D],
                                              qkv[:, b.buf, tile, 2 * C:3 * C].rearrange("p (h d) -> p h d", d=D)
                                              ).then_inc(v_done, 1)
                b = t + 3
                if b.within(B):
                    pool.wait_ge(gate_steps, 10 * (b.n + 1))
                    newton(ln_newton, 12, 12 * b.n, ln_y[:, :], ln_v[:, :], ln_t[:, :])
                b = t + 4
                if b.within(B):
                    pool.wait_ge(rank_done, TC * (b.n + 1))
                    held(pool, gathered, b.n - 1, spare)
                    for c in range(TC):
                        nc.gpsimd.tensor_scalar(onehot[:, b.buf, c, :], place[:, :], rank[:, b.buf, c:c + 1],
                                                None, ALU.is_equal).then_inc(onehot_done, 1)
                b = t + 2
                if b.within(B):
                    held(pool, stack_hi, b.n + 1, spare)
                    sv = stack[:, b.buf, :, :, :, :]
                    for half in range(2):
                        nc.gpsimd.tensor_copy(sv[:, half, 0, :, 8:16], sv[:, half, 0, :, 0:8]).then_inc(stack_pool, 1)
                        nc.gpsimd.tensor_copy(sv[:, half, 1, :, 16:24], sv[:, half, 1, :, 0:8]).then_inc(stack_pool, 1)
                    nc.gpsimd.memset(sv[:, :, 0, :, 24:25].rearrange("p t h o -> p t (h o)"), 0.0).then_inc(stack_pool, 1)

            pool.wait_ge(const_dve, CONST_DVE)
            pool.wait_ge(const_act, CONST_ACT)
            steps(pool, step)

            def bc(v):
                return v.rearrange("p (t o) -> p t o", o=1).broadcast_to([HALF, CT, C])

            def rows(v):
                return v.rearrange("p (o f) -> p o f", o=1).broadcast_to([HALF, CT, C])

            def chunk(c):
                b = c + 2
                if not b.within(NCH):
                    return
                at = 31 * b.n
                h4 = hsel[:, bass.ds(b.n * CB, CB), :, :].rearrange("p b t f -> p (b t) f")
                for again in range(2):
                    pool.wait_ge(n_stat, 38 * b.n + 19 * (again + 1))
                    newton(n_pool, 13, at + 14 * again, n_y[:, :], n_v[:, :], n_t[:, :])
                    src = h4 if again == 0 else n_x[:, :, :]
                    nc.gpsimd.tensor_tensor(n_z[:, :, :], src, bc(n_mv[:, :, 0]), ALU.subtract).then_inc(n_pool, 1)
                    pool.wait_ge(n_pool, at + 14 * again + 13)
                    if again == 0:
                        nc.gpsimd.tensor_tensor(n_x[:, :, :], n_z[:, :, :], bc(n_y[:, :]), ALU.mult).then_inc(n_pool, 1)
                        pool.wait_ge(n_pool, at + 14)
                    else:
                        nc.gpsimd.tensor_tensor(n_z[:, :, :], n_z[:, :, :], bc(n_y[:, :]), ALU.mult).then_inc(n_pool, 1)
                        pool.wait_ge(n_pool, at + 28)
                nc.gpsimd.tensor_tensor(n_z[:, :, :], n_z[:, :, :], rows(gam[:, :]), ALU.mult).then_inc(n_pool, 1)
                pool.wait_ge(n_pool, at + 29)
                passed(pool, n_hi, b.n)
                nc.gpsimd.tensor_tensor(n_x[:, :, :], n_z[:, :, :], rows(bet[:, :]), ALU.add).then_inc(n_pool, 1)
                pool.wait_ge(n_pool, at + 30)
                pool.wait_ge(n_hi, b.n + 1)
                nc.gpsimd.tensor_tensor(xs[:, :, C:2 * C], n_x[:, :, :], xs[:, :, 0:C],
                                        ALU.subtract).then_inc(n_pool, 1)

            pool.wait_ge(h_done, B)
            chunk_steps(pool, chunk)

        @block.scalar
        def _(act):
            for half in range(2):
                act.dma_start(w_raw[:, half, :], qkv_w[half * META:(half + 1) * META, :]).then_inc(c_qkvw, 16)
            act.dma_start(w_qkv[C:C + 1, :], qkv_b.rearrange("(o n) -> o n", o=1)).then_inc(c_qkvb, 16)
            act.dma_start(wp_raw[:, :], proj_w).then_inc(c_projw, 16)
            act.dma_start(w_proj[C:C + 1, :], proj_b.rearrange("(o n) -> o n", o=1)).then_inc(c_projb, 16)
            act.dma_start(ls[:, :], logit_scale.rearrange("(o n) -> o n", o=1).broadcast_to([HALF, H])).then_inc(c_ls, 16)
            act.dma_start(rel[:, :], rel_log).then_inc(c_rel, 16)
            act.dma_start(m1t[:, :], mlp1_w.rearrange("m c -> c m"), allow_slow_non_contiguous=True).then_inc(c_mlp, 16)
            act.dma_start(m1b[:, :], mlp1_b.rearrange("(m o) -> m o", o=1)).then_inc(c_mlp, 16)
            act.dma_start(m2t[:, :], mlp2_w.rearrange("h m -> m h"), allow_slow_non_contiguous=True).then_inc(c_mlp, 16)
            act.dma_start(m2b[:, :], mlp2_b.rearrange("(o n) -> o n", o=1).broadcast_to([128, H])).then_inc(c_mlp, 16)
            act.wait_ge(c_mlp, 64)
            for r in range(2):
                act.wait_ge(const_pe, r + 1)
                nc.scalar.activation(hid[:, r * REL:(r + 1) * REL], s1[0:META, 512 * r:512 * r + REL], ACT.Relu,
                                     bias=m1b[:, :]).then_inc(const_act, 1)
            act.wait_ge(const_pe, 5)
            nc.scalar.activation(w_qkv[0:C, 0:META], MA[0:C, 0:META], ACT.Copy).then_inc(const_act, 1)
            nc.scalar.activation(w_qkv[0:C, META:2 * META], MA[0:C, META:2 * META], ACT.Copy).then_inc(const_act, 1)
            nc.scalar.activation(w_proj[0:C, :], MA[0:C, 192:192 + C], ACT.Copy).then_inc(const_act, 1)
            act.wait_ge(const_dve, 1)
            for half in range(2):
                nc.scalar.activation(qk_scale[:, half, 0, :], ls[:, :], ACT.Exp).then_inc(const_act, 1)
            act.wait_ge(const_dve, 2)
            for n in range(2 * H):
                r, h = n // H, n % H
                act.wait_ge(const_pe, 6 + n)
                nc.scalar.activation(dist[:, r, h, :], s2[0:HALF, 512 * (n % 4):512 * (n % 4) + REL], ACT.Identity,
                                     bias=m2bs[0:HALF, h:h + 1], scale=KSCALE).then_inc(const_act, 1)
            act.dma_start(w1raw[0:C, :, :], W1.rearrange("e d h -> d e h")).then_inc(c_moe, 16)
            act.dma_start(w1raw[C:2 * C, :, :], W1.rearrange("e d h -> d e h")).then_inc(c_moe, 16)
            act.dma_start(wr_raw[0:C, :], Wr).then_inc(c_moe, 16)
            act.dma_start(wr_raw[C:2 * C, :], Wr).then_inc(c_moe, 16)
            act.dma_start(w2[:, :, :], W2.rearrange("e h d -> h e d")).then_inc(c_moe, 16)
            act.dma_start(b1raw[:, :], b1).then_inc(c_moe, 16)
            act.dma_start(b2raw[:, :], b2.rearrange("(o e) d -> o (e d)", o=1)).then_inc(c_moe, 16)
            act.dma_start(br_b[:, :], br.rearrange("(o n) -> o n", o=1).broadcast_to([HALF, E])).then_inc(c_moe, 16)
            act.dma_start(gam[:, :], gamma.rearrange("(o n) -> o n", o=1).broadcast_to([HALF, C])).then_inc(c_moe, 16)
            act.dma_start(bet[:, :], beta.rearrange("(o n) -> o n", o=1).broadcast_to([HALF, C])).then_inc(c_moe, 16)
            act.wait_ge(const_dve, 5)
            act.dma_start(bias_dram.rearrange("r h p w -> p (r h) w"),
                          dist16.rearrange("p r h w -> p (r h) w")).then_inc(bias_stored, 16)

            def exps(b, u):
                if not b.within(B):
                    return
                g, tile = u // 2, u % 2
                rows = HALF - tile
                act.wait_ge(s2_ready, 4 * b.n + u + 1)
                passed(act, pv_done, 4 * (b.n - 1) + u + 1)
                sv = s2[0:rows, 1024 * (u % 2):1024 * (u % 2) + 1024].rearrange("p (k c) -> p k c", k=2)[:, :, 0:2 * LQ]
                nc.scalar.activation(P[0:rows, u, :, :].rearrange("p (k j) l -> p k (j l)", k=2), sv, ACT.Exp,
                                     scale=1.0 / KSCALE).then_inc(exp_done, 1)

            def step(t):
                b = t
                if b.within(B):
                    act.wait_ge(t2_ready, b.n + 1)
                    passed(act, s2_ready, 4 * b.n)
                    nc.scalar.activation(qT2[:, :, :], MA16[:, 0:2 * LQ].rearrange("p (g l) -> p g l", g=2),
                                         ACT.Copy).then_inc(t2_out, 1)
                b = t + 1
                if b.within(B):
                    act.wait_ge(t1_ready, b.n + 1)
                    passed(act, s1_ready, 8 * b.n)
                    nc.scalar.activation(qT1[:, :, :], MA16[:, 0:2 * LQ].rearrange("p (g l) -> p g l", g=2),
                                         ACT.Copy).then_inc(t1_out, 1)
                    passed(act, s2_ready, 4 * (b.n - 1))
                    for hh in range(4):
                        q = slice(32 * hh, 32 * hh + 32)
                        nc.scalar.activation(kT[q, b.buf, :, hh, :],
                                             MA16[q, 2 * LQ:4 * LQ].rearrange("p (g l) -> p g l", g=2),
                                             ACT.Copy).then_inc(t1_out, 1)
                b = t + (-1)
                if b.within(B):
                    act.wait_ge(pv_done, 4 * (b.n + 1))
                    passed(act, to_ready, b.n)
                    nc.scalar.activation(oT[:, :, :], MB[:, 0:2 * LQ].rearrange("p (g l) -> p g l", g=2),
                                         ACT.Copy).then_inc(oT_out, 1)
                exps(t, 0)
                b = t + 3
                if b.within(B):
                    act.wait_ge(gathered, b.n + 1)
                    passed(act, gate_steps, 10 * b.n)
                    nc.scalar.activation(sel[:, :, :], MA[0:HALF, 0:2 * (C + 1)].rearrange("p (t f) -> p t f", t=2),
                                         ACT.Copy).then_inc(sel_out, 1)
                    act.wait_ge(sel_out, 2 * b.n + 1)
                    nc.scalar.activation(egate[:, :], sel[:, :, C], ACT.Exp, scale=-1.0).then_inc(sel_out, 1)
                b = t + 2
                if b.within(B):
                    act.wait_ge(stack_dve, 3 * b.n + 1)
                    passed(act, t2_ready, b.n - 1)
                    nc.scalar.activation(stack[:, b.buf, :, :, :, 0:D].rearrange("p t q h d -> p (t q h) d"),
                                         qn[:, :, :].rearrange("p t (g d) -> p (t g) d", d=D),
                                         ACT.Copy).then_inc(stack_hi, 1)
                exps(t, 1)
                b = t + (-1)
                if b.within(B):
                    act.wait_ge(onT_ready, b.n + 1)
                    passed(act, pr_ready, b.n)
                    nc.scalar.activation(onT[0:C, :], MB[0:C, 0:LQ], ACT.Copy).then_inc(onT_out, 1)
                exps(t, 2)
                b = t + 3
                if b.within(B):
                    act.wait_ge(xnT_ready, b.n + 1)
                    passed(act, qkv_ready, b.n)
                    nc.scalar.activation(xnT[0:C, :], MA[0:C, 0:LQ], ACT.Copy).then_inc(xnT_out, 1)
                exps(t, 3)
                if b.within(B):
                    act.wait_ge(qkv_ready, b.n + 1)
                    passed(act, v_done, 2 * (b.n - 1))
                    passed(act, stack_dve, 3 * (b.n - 2) + 1)
                    pv = MA[0:HALF, 0:6 * C].rearrange("p (t f) -> p t f", t=2)
                    nc.scalar.activation(qkv[:, b.buf, :, :], pv, ACT.Copy).then_inc(qkv_out, 1)
                    passed(act, norm_steps, 4 * (b.n - 1) + 1)
                    nc.scalar.activation(sq[:, :, :], pv[:, :, 0:2 * C], ACT.Square).then_inc(qkv_out, 1)

            steps(act, step)

            act.wait_ge(const_pe, 22)
            nc.scalar.activation(b1c[:, :], MB[:, 0:E], ACT.Copy).then_inc(const_act, 1)
            act.wait_ge(const_act, CONST_ACT + 1)

            def chunk(c):
                b = c + 2
                layer = c + 1
                for e in range(E):
                    if layer.within(NCH):
                        act.wait_ge(h_ready, E * layer.n + e + 1)
                        if e == 0:
                            passed(act, y_ready, CT * (layer.n - 1))
                        hv = s2[:, 1024 * (e % 2):1024 * (e % 2) + 1024].rearrange("p (k c) -> p k c", k=2)[:, :, 0:376]
                        nc.scalar.activation(hT[:, layer.buf, e, :].rearrange("p (k c) -> p k c", k=2), hv, ACT.Gelu,
                                             bias=b1c[:, e:e + 1], scale=1.0 / WSCALE).then_inc(gelu_done, 1)
                    if e == 5 and b.within(NCH):
                        act.wait_ge(n_pool, 31 * b.n + 30)
                        passed(act, xsT_ready, b.n)
                        nc.scalar.activation(xs[:, :, 0:C], n_x[:, :, :], ACT.Copy).then_inc(n_hi, 1)
                if b.within(NCH):
                    act.wait_ge(xsT_ready, b.n + 1)
                    passed(act, h_ready, E * (b.n - 1))
                    passed(act, lg_ready, b.n - 1)
                    nc.scalar.activation(xsT[:, b.buf, :], MA16[:, 0:CT * HALF], ACT.Copy).then_inc(xsT_out, 1)
                    act.wait_ge(gates, 16 * b.n + 13)
                    nc.scalar.activation(th[:, :], dif[:, :], ACT.Tanh, scale=0.5).then_inc(th_done, 1)

            chunk_steps(act, chunk)

        @block.vector
        def _(dve):
            nc.vector.memset(bias_q[64:128, :, :, :], 0.0)
            nc.vector.memset(bias_k[64:128, :, :, :, :], 0.0)
            dve.wait_ge(c_ls, 16)
            nc.vector.tensor_scalar(ls[:, :], ls[:, :], LOG100, None, ALU.min).then_inc(const_dve, 1)
            dve.wait_ge(c_mlp, 64)
            nc.vector.tensor_scalar(m2bs[:, :], m2b[:, :], KSCALE, None, ALU.mult)
            nc.vector.tensor_copy(m2rep[:, :, :], m2t[:, :].rearrange("p (h o) -> p h o", o=1)
                                  .broadcast_to([META, H, 128])).then_inc(const_dve, 1)
            dve.wait_ge(const_act, 7 + 2 * H)
            nc.vector.tensor_copy(dist16[:, 0, :, :], dist[:, 0, :, :]).then_inc(const_dve, 1)
            nc.vector.tensor_copy(dist16[:, 2, :, :], dist[:, 1, :, :]).then_inc(const_dve, 1)
            dve.wait_ge(const_dve, 3)
            nc.vector.tensor_tensor(dist16[:, 1, :, :], dist[:, 0, :, :], dist16[:, 0, :, :],
                                    ALU.subtract).then_inc(const_dve, 1)
            dve.wait_ge(const_pool, 8)
            nc.vector.tensor_copy(ident16[:, :], ident[:, :])
            nc.vector.tensor_copy(place[:, :], place_i[:, :])
            nc.vector.tensor_copy(prio[:, :], prio_i[:, :])
            nc.vector.memset(qk_scale[:, :, 1, :], KSCALE)
            nc.vector.memset(xnT[C:C + 1, :], 1.0)
            nc.vector.memset(onT[C:C + 1, :], 1.0)
            nc.vector.memset(ones16[:, :], 1.0)
            nc.vector.memset(kT[:, :, :, :, :], 0.0)
            nc.vector.memset(V[:, :, :, :, :], 0.0)
            nc.vector.memset(P[:, :, :, :], 0.0)
            nc.vector.memset(stack[:, :, :, :, :, :], 0.0).then_inc(const_dve, 1)
            dve.wait_ge(const_dve, 6)
            nc.vector.memset(stack[:, :, :, 1, :, 24:25].rearrange("p b t h o -> p (b t) (h o)"), 1.0)
            nc.vector.memset(V[0:HALF, :, :, :, D:D + 1].rearrange("p b t h o -> p (b t) (h o)"), 1.0).then_inc(const_dve, 1)

            def split_max(b, n):
                if not b.within(B):
                    return
                half, j = n // 4, n % 4
                dve.wait_ge(s1_ready, 8 * b.n + n + 1)
                nc.vector.tensor_reduce(stack[:, b.buf, half, 0, 2 * j:2 * j + 2, 24:25],
                                        s1[0:HALF, 512 * (n % 2):512 * (n % 2) + 2 * NSEL].rearrange("p (h m) -> p h m", h=2),
                                        AX.X, ALU.max, negate=True).then_inc(neg_max, 1)

            def step(t):
                b = t + 4
                if b.within(B):
                    dve.wait_ge(x_loaded[b.buf], 16 * (b.turn + 1))
                    nc.vector.tensor_tensor(prod[:, :, :], X[:, b.buf, :, 0:C],
                                            wscore[:, :].rearrange("p (o f) -> p o f", o=1).broadcast_to([TP, TC, C]),
                                            ALU.mult).then_inc(score, 1)
                    dve.wait_ge(score, 2 * b.n + 1)
                    passed(dve, gathered, b.n - 1)
                    nc.vector.tensor_reduce(X[:, b.buf, :, C:C + 1], prod[:, :, :], AX.X, ALU.add).then_inc(score, 1)
                b = t + 2
                if b.within(B):
                    dve.wait_ge(qk_newton, 13 * (b.n + 1))
                    passed(dve, stack_hi, b.n)
                    nc.vector.tensor_tensor(qn[:, :, :].rearrange("p t (g d) -> p t g d", d=D),
                                            qkv[:, b.buf, :, 0:2 * C].rearrange("p t (g d) -> p t g d", d=D),
                                            nt[:, :].rearrange("p (t g o) -> p t g o", t=2, o=1).broadcast_to([HALF, 2, 2 * H, D]),
                                            ALU.mult).then_inc(stack_dve, 1)
                split_max(t + 1, 0)
                split_max(t + 1, 1)
                if b.within(B):
                    dve.wait_ge(stack_hi, b.n + 1)
                    for qk, at in ((0, 16), (1, 8)):
                        nc.vector.tensor_tensor(stack[:, b.buf, :, qk, :, at:at + D],
                                                qn[:, :, qk * C:(qk + 1) * C].rearrange("p t (h d) -> p t h d", d=D),
                                                stack[:, b.buf, :, qk, :, 0:D], ALU.subtract).then_inc(stack_dve, 1)
                b = t + 3
                if b.within(B):
                    k = 10 * b.n
                    dve.wait_ge(sel_out, 2 * (b.n + 1))
                    nc.vector.tensor_scalar(egate[:, :], egate[:, :], 1.0, None, ALU.add).then_inc(gate_steps, 1)
                    dve.wait_ge(gate_steps, k + 1)
                    nc.vector.reciprocal(gate[:, :], egate[:, :]).then_inc(gate_steps, 1)
                    dve.wait_ge(gate_steps, k + 2)
                    hb = hsel[:, bass.ds(b.n, 1), :, :].rearrange("p o t f -> p (o t) f")
                    nc.vector.tensor_tensor(hb, sel[:, :, 0:C],
                                            gate[:, :].rearrange("p (t o) -> p t o", o=1).broadcast_to([HALF, 2, C]),
                                            ALU.mult).then_inc(gate_steps, 1)
                    held(dve, gate_steps, k + 3, spare)
                    for half in range(2):
                        nc.vector.bn_stats(stats[:, half, :], hb[:, half, :]).then_inc(gate_steps, 1)
                    dve.wait_ge(gate_steps, k + 5)
                    held(dve, xn_done, 2 * b.n, spare)
                    for half in range(2):
                        nc.vector.bn_aggr(mv[:, half, :], stats[:, half, :]).then_inc(gate_steps, 1)
                    dve.wait_ge(gate_steps, k + 7)
                    nc.vector.tensor_scalar(ln_v[:, :], mv[:, :, 1], EPS, None, ALU.add).then_inc(gate_steps, 1)
                    dve.wait_ge(gate_steps, k + 8)
                    nc.vector.tensor_scalar(ln_i[:, :], ln_v[:, :].bitcast(i32), 1, None,
                                            ALU.logical_shift_right).then_inc(gate_steps, 1)
                    dve.wait_ge(gate_steps, k + 9)
                    nc.vector.tensor_scalar(ln_y[:, :].bitcast(i32), ln_i[:, :], -1.0, MAGIC, ALU.mult,
                                            ALU.add).then_inc(gate_steps, 1)
                b = t + (-1)
                if b.within(B):
                    dve.wait_ge(to_ready, b.n + 1)
                    to = MB[0:HALF, :].rearrange("p (g w) -> p g w", w=QW)
                    nc.vector.reciprocal(rz[:, :].rearrange("p (g o) -> p g o", o=1), to[:, :, D:D + 1]).then_inc(on_done, 1)
                    dve.wait_ge(on_done, 2 * b.n + 1)
                    nc.vector.tensor_tensor(on[:, :, :].rearrange("p t (g d) -> p (t g) d", d=D), to[:, :, 0:D],
                                            rz[:, :].rearrange("p (g o) -> p g o", o=1).broadcast_to([HALF, 16, D]),
                                            ALU.mult).then_inc(on_done, 1)
                split_max(t + 1, 2)
                split_max(t + 1, 3)
                b = t + 4
                if b.within(B):
                    dve.wait_ge(ranks_row, b.n + 1)
                    passed(dve, onehot_done, TC * (b.n - 1))
                    passed(dve, rank_done, TC * b.n)
                    for c in range(TC):
                        nc.vector.scalar_tensor_tensor(flags[:, c, :], MA[0:TP, 0:N], X[:, b.buf, c, C:C + 1],
                                                       before[:, c, :], ALU.subtract, ALU.is_gt,
                                                       accum_out=rank[:, b.buf, c:c + 1]).then_inc(rank_done, 1)
                split_max(t + 1, 4)
                split_max(t + 1, 5)
                b = t + 3
                if b.within(B):
                    dve.wait_ge(ln_newton, 12 * (b.n + 1))
                    passed(dve, xnT_ready, b.n)
                    for half in range(2):
                        nc.vector.tensor_scalar(xn[:, half, :], hsel[:, bass.ds(b.n, 1), half, :].rearrange("p o f -> p (o f)"),
                                                mv[:, half, 0:1], ln_y[:, half:half + 1], ALU.subtract,
                                                ALU.mult).then_inc(xn_done, 1)
                split_max(t + 1, 6)
                split_max(t + 1, 7)
                b = t + (-1)
                if b.within(B):
                    dve.wait_ge(pr_ready, b.n + 1)
                    hb = hsel[:, bass.ds(b.n, 1), :, :].rearrange("p o t f -> p (o t f)")
                    nc.vector.tensor_tensor(hb, hb, MB[0:HALF, 0:2 * C], ALU.add).then_inc(h_done, 1)
                b = t + 3
                if b.within(B):
                    dve.wait_ge(qkv_out, 2 * (b.n + 1))
                    passed(dve, qk_newton, 13 * b.n)
                    nc.vector.tensor_reduce(nv[:, :].rearrange("p (g o) -> p g o", o=1),
                                            sq[:, :, :].rearrange("p t (g d) -> p (t g) d", d=D), AX.X,
                                            ALU.add).then_inc(norm_steps, 1)
                    dve.wait_ge(norm_steps, 4 * b.n + 1)
                    nc.vector.tensor_scalar(nv[:, :], nv[:, :], 1e-24, None, ALU.max).then_inc(norm_steps, 1)
                    dve.wait_ge(norm_steps, 4 * b.n + 2)
                    nc.vector.tensor_scalar(ni[:, :], nv[:, :].bitcast(i32), 1, None,
                                            ALU.logical_shift_right).then_inc(norm_steps, 1)
                    dve.wait_ge(norm_steps, 4 * b.n + 3)
                    nc.vector.tensor_scalar(ny[:, :].bitcast(i32), ni[:, :], -1.0, MAGIC, ALU.mult,
                                            ALU.add).then_inc(norm_steps, 1)

            dve.wait_ge(c_wscore, 16)
            steps(dve, step)

            dve.wait_ge(c_moe, 160)
            nc.vector.tensor_scalar(w1raw[:, :, :], w1raw[:, :, :], WSCALE, None, ALU.mult)
            nc.vector.tensor_scalar(wr_raw[:, :], wr_raw[:, :], WSCALE, None, ALU.mult).then_inc(const_dve, 1)
            dve.wait_ge(const_dve, CONST_DVE + 1)
            nc.vector.tensor_copy(w1s[:, :, 0, :], w1raw[:, :, :])
            nc.vector.tensor_copy(wrs[:, 0, :], wr_raw[:, :])
            nc.vector.tensor_copy(b2hl[:, 0, :], b2raw[:, :]).then_inc(const_dve, 1)
            dve.wait_ge(const_dve, CONST_DVE + 2)
            nc.vector.tensor_tensor(w1s[:, :, 1, :], w1raw[:, :, :], w1s[:, :, 0, :], ALU.subtract)
            nc.vector.tensor_tensor(wrs[:, 1, :], wr_raw[:, :], wrs[:, 0, :], ALU.subtract)
            nc.vector.tensor_tensor(b2hl[:, 1, :], b2raw[:, :], b2hl[:, 0, :], ALU.subtract).then_inc(const_dve, 1)
            dve.wait_ge(h_done, B)

            def guess(b, again):
                k = 38 * b.n + 19 * again
                src = (hsel[:, bass.ds(b.n * CB, CB), :, :].rearrange("p b t f -> p (b t) f")
                       if again == 0 else n_x[:, :, :])
                for j in range(CT):
                    nc.vector.bn_stats(n_stats[:, j, :], src[:, j, :]).then_inc(n_stat, 1)
                held(dve, n_stat, k + 8, spare)
                for j in range(CT):
                    nc.vector.bn_aggr(n_mv[:, j, :], n_stats[:, j, :]).then_inc(n_stat, 1)
                dve.wait_ge(n_stat, k + 16)
                nc.vector.tensor_scalar(n_v[:, :], n_mv[:, :, 1], EPS, None, ALU.add).then_inc(n_stat, 1)
                dve.wait_ge(n_stat, k + 17)
                nc.vector.tensor_scalar(n_i[:, :], n_v[:, :].bitcast(i32), 1, None,
                                        ALU.logical_shift_right).then_inc(n_stat, 1)
                dve.wait_ge(n_stat, k + 18)
                nc.vector.tensor_scalar(n_y[:, :].bitcast(i32), n_i[:, :], -1.0, MAGIC, ALU.mult,
                                        ALU.add).then_inc(n_stat, 1)

            def combine(c, j):
                if not c.within(NCH):
                    return
                k = 24 * c.n + 3 * j
                if j == 0:
                    dve.wait_ge(gates, 16 * (c.n + 1))
                dve.wait_ge(y_ready, CT * c.n + j + 1)
                nc.vector.tensor_tensor(yw[:, j % 2, :, :],
                                        s1[0:HALF, 512 * (j % 2):512 * (j % 2) + 512].rearrange("p (e d) -> p e d", e=E),
                                        wfull[:, c.buf, j, :].rearrange("p (e o) -> p e o", o=1).broadcast_to([HALF, E, C]),
                                        ALU.mult).then_inc(y_dve, 1)
                dve.wait_ge(y_dve, k + 1)
                nc.vector.tensor_reduce(yr[:, j % 2, :].rearrange("p (d o) -> p d o", o=1),
                                        yw[:, j % 2, :, :].rearrange("p e d -> p d e"), AX.X, ALU.add).then_inc(y_dve, 1)
                dve.wait_ge(y_dve, k + 2)
                hb = hsel[:, bass.ds(c.n * CB + j // 2, 1), j % 2, :].rearrange("p o f -> p (o f)")
                nc.vector.tensor_tensor(yo[:, c.buf, j, :], yr[:, j % 2, :], hb, ALU.add).then_inc(y_dve, 1)

            def b8(v):
                return v.rearrange("p (t o) -> p t o", o=1).broadcast_to([HALF, CT, E])

            def over_e(v):
                return v.rearrange("p (o e) -> p o e", o=1).broadcast_to([HALF, CT, E])

            def chunk(c):
                b = c + 2
                if b.within(NCH):
                    held(dve, n_pool, 31 * b.n, spare)
                    guess(b, 0)
                if c.within(NCH):
                    passed(dve, out_done[c.buf], 32 * c.turn)
                for j in range(3):
                    combine(c, j)
                if b.within(NCH):
                    held(dve, n_pool, 31 * b.n + 14, spare)
                    guess(b, 1)
                for j in range(3, 8):
                    combine(c, j)
                if b.within(NCH):
                    k = 16 * b.n
                    dve.wait_ge(lg_ready, b.n + 1)
                    nc.vector.scalar_tensor_tensor(lg[:, :, :], MA[0:HALF, 0:CT * E].rearrange("p (t e) -> p t e", e=E),
                                                   1.0 / WSCALE, over_e(br_b[:, :]), ALU.mult, ALU.add).then_inc(gates, 1)
                    for r, (src, top, oh) in enumerate(((lg, top1, oh1), (lg2, top2, oh2))):
                        k += 6 * r
                        dve.wait_ge(gates, k + 1)
                        nc.vector.tensor_reduce(top[:, :].rearrange("p (t o) -> p t o", o=1), src[:, :, :], AX.X,
                                                ALU.max).then_inc(gates, 1)
                        dve.wait_ge(gates, k + 2)
                        nc.vector.tensor_tensor(eq[:, :, :], src[:, :, :], b8(top[:, :]), ALU.is_equal).then_inc(gates, 1)
                        dve.wait_ge(gates, k + 3)
                        nc.vector.tensor_tensor(eq[:, :, :], eq[:, :, :], over_e(prio[:, :]), ALU.mult).then_inc(gates, 1)
                        dve.wait_ge(gates, k + 4)
                        nc.vector.tensor_reduce(pick[:, :].rearrange("p (t o) -> p t o", o=1), eq[:, :, :], AX.X,
                                                ALU.max).then_inc(gates, 1)
                        dve.wait_ge(gates, k + 5)
                        nc.vector.tensor_tensor(oh[:, :, :], eq[:, :, :], b8(pick[:, :]), ALU.is_equal).then_inc(gates, 1)
                        dve.wait_ge(gates, k + 6)
                        if r == 0:
                            nc.vector.scalar_tensor_tensor(lg2[:, :, :], oh1[:, :, :], -1e30, lg[:, :, :], ALU.mult,
                                                           ALU.add).then_inc(gates, 1)
                    nc.vector.tensor_tensor(dif[:, :], top1[:, :], top2[:, :], ALU.subtract).then_inc(gates, 1)
                    k = 16 * b.n + 13
                    dve.wait_ge(th_done, b.n + 1)
                    nc.vector.tensor_scalar(wa[:, :], th[:, :], 0.5, 0.5, ALU.mult, ALU.add)
                    nc.vector.tensor_scalar(wb[:, :], th[:, :], -0.5, 0.5, ALU.mult, ALU.add).then_inc(gates, 1)
                    dve.wait_ge(gates, k + 1)
                    nc.vector.tensor_tensor(oh1[:, :, :], oh1[:, :, :], b8(wa[:, :]), ALU.mult)
                    nc.vector.tensor_tensor(oh2[:, :, :], oh2[:, :, :], b8(wb[:, :]), ALU.mult).then_inc(gates, 1)
                    dve.wait_ge(gates, k + 2)
                    nc.vector.tensor_tensor(wfull[:, b.buf, :, :], oh1[:, :, :], oh2[:, :, :], ALU.add).then_inc(gates, 1)

            chunk_steps(dve, chunk)

        @block.tensor
        def _(pe):
            mm = nc.tensor.matmul
            pe.wait_ge(c_rel, 16)
            pe.wait_ge(c_mlp, 64)
            for r in range(2):
                mm(s1[0:META, 512 * r:512 * r + REL], m1t[:, :], rel[:, r * REL:(r + 1) * REL], start=True,
                   stop=True).then_inc(const_pe, 1)
            pe.wait_ge(const_pool, 5)
            pe.wait_ge(c_qkvw, 32)
            pe.wait_ge(c_projw, 16)
            for r in range(2):
                nc.tensor.transpose(MA[0:C, r * META:(r + 1) * META], w_raw[:, r, :], ident[0:META, 0:META]).then_inc(const_pe, 1)
            nc.tensor.transpose(MA[0:C, 192:192 + C], wp_raw[:, :], ident[0:C, 0:C]).then_inc(const_pe, 1)
            pe.wait_ge(const_act, 2)
            pe.wait_ge(const_dve, 2)
            for n in range(2 * H):
                r, h = n // H, n % H
                if n >= 4:
                    pe.wait_ge(const_act, 7 + n - 3)
                mm(s2[:, 512 * (n % 4):512 * (n % 4) + REL], m2rep[:, h, :], hid[:, r * REL:(r + 1) * REL], start=True,
                   stop=True).then_inc(const_pe, 1)

            def row_max(b, n):
                if not b.within(B):
                    return
                half, j = n // 4, n % 4
                g, hh = j // 2, 2 * (j % 2)
                if n == 0:
                    pe.wait_ge(t1_out, 5 * (b.n + 1))
                passed(pe, neg_max, 8 * b.n + n - 1)
                o = s1[0:HALF, 512 * (n % 2):512 * (n % 2) + 2 * NSEL]
                mm(o, ident16[:, 0:HALF], bias_q[:, half, 2 * j:2 * j + 2, :].rearrange("p h m -> p (h m)"),
                   start=True, stop=False)
                mm(o.rearrange("p (h m) -> p h m", h=2), qT1[:, g, half * HALF:(half + 1) * HALF],
                   kT[:, b.buf, g, hh:hh + 2, 0:NSEL], start=False, stop=True).then_inc(s1_ready, 1)

            def logits(b, u):
                if not b.within(B):
                    return
                g, tile = u // 2, u % 2
                rows = HALF - tile
                if u == 0:
                    pe.wait_ge(t2_out, b.n + 1)
                passed(pe, exp_done, 4 * b.n + u - 1)
                for k in range(2):
                    at = 1024 * (u % 2) + 512 * k
                    h0 = 4 * g + 2 * k
                    o = s2[0:rows, at:at + 2 * LQ]
                    for part in range(2):
                        mm(o, ident16[:, 0:rows], bias_k[:, tile, part, h0:h0 + 2, :].rearrange("p h l -> p (h l)"),
                           start=part == 0, stop=part == 1)
                    for j in range(2):
                        last = mm(s2[0:rows, at + j * LQ:at + (j + 1) * LQ],
                                  kT[:, b.buf, g, 2 * k + j, tile * HALF:tile * HALF + rows], qT2[:, g, :],
                                  start=False, stop=True, skip_group_check=True)
                last.then_inc(s2_ready, 1)

            def weigh(b, u):
                if not b.within(B):
                    return
                g, tile = u // 2, u % 2
                pe.wait_ge(exp_done, 4 * b.n + u + 1)
                if u == 0:
                    pe.wait_ge(v_done, 2 * (b.n + 1))
                    passed(pe, h_done, b.n)
                for hh in range(4):
                    last = mm(MB[32 * hh:32 * hh + QW, g * LQ:(g + 1) * LQ], V[:, b.buf, tile, 4 * g + hh, :],
                              P[:, u, hh, :], start=tile == 0, stop=tile == 1, tile_position=(0, 32 * hh),
                              skip_group_check=True)
                last.then_inc(pv_done, 1)

            def step(t):
                if t.within(B):
                    b = t
                    pe.wait_ge(neg_max, 8 * (b.n + 1))
                    if (t + 1).within(B):
                        pe.wait_ge(qkv_out, 2 * (b.n + 3) if (t + 2).within(B) else 2 * B)
                    for g in range(2):
                        for half in range(2):
                            last = nc.tensor.transpose(MA16[:, g * LQ + half * HALF:g * LQ + (half + 1) * HALF],
                                                       stack[:, b.buf, half, 0, 4 * g:4 * g + 4, :].rearrange("p h w -> p (h w)"),
                                                       ident16[0:HALF, 0:HALF])
                    last.then_inc(t2_ready, 1)
                weigh(t + (-1), 3)
                b = t + 1
                if b.within(B):
                    pe.wait_ge(stack_dve, 3 * (b.n + 1))
                    pe.wait_ge(stack_pool, 5 * (b.n + 1))
                    if (b + 2).within(B):
                        pe.wait_ge(qkv_out, 2 * (b.n + 2))
                    passed(pe, t2_out, b.n)
                    for qk in range(2):
                        for g in range(2):
                            for half in range(2):
                                at = (2 * qk + g) * LQ + half * HALF
                                last = nc.tensor.transpose(MA16[:, at:at + HALF],
                                                           stack[:, b.buf, half, qk, 4 * g:4 * g + 4, :].rearrange("p h w -> p (h w)"),
                                                           ident16[0:HALF, 0:HALF])
                    last.then_inc(t1_ready, 1)
                logits(t, 0)
                b = t + 3
                if b.within(B):
                    pe.wait_ge(onehot_done, TC * (b.n + 1))
                    if (t + 1).within(B):
                        pe.wait_ge(t1_out, 5 * (t.n + 2))
                    elif (t + 2).within(B):
                        pe.wait_ge(qkv_out, 2 * (t.n + 3))
                    for half in range(2):
                        for c in range(TC):
                            last = mm(MA[0:HALF, half * (C + 1):(half + 1) * (C + 1)],
                                      onehot[:, b.buf, c, half * HALF:(half + 1) * HALF], X[:, b.buf, c, :],
                                      start=c == 0, stop=c == TC - 1)
                    last.then_inc(gathered, 1)
                row_max(t + 1, 0)
                row_max(t + 1, 1)
                b = t + (-1)
                if b.within(B):
                    pe.wait_ge(oT_out, b.n + 1)
                    for half in range(2):
                        for g in range(2):
                            last = nc.tensor.transpose(MB[0:HALF, (2 * half + g) * 128:(2 * half + g + 1) * 128],
                                                       oT[:, g, half * HALF:(half + 1) * HALF], ident[:, :])
                    last.then_inc(to_ready, 1)
                b = t + 4
                if b.within(B):
                    pe.wait_ge(score, 2 * (b.n + 1))
                    passed(pe, sel_out, 2 * b.n - 1)
                    for c in range(TC):
                        last = nc.tensor.transpose(MA[0:TP, c * TP:(c + 1) * TP],
                                                   X[:, b.buf, c, C:C + 1].broadcast_to([TP, TP]), ident[0:TP, 0:TP])
                    last.then_inc(ranks_row, 1)
                logits(t, 1)
                row_max(t + 1, 2)
                row_max(t + 1, 3)
                b = t + (-1)
                if b.within(B):
                    held(pe, on_done, 2 * (b.n + 1), spare)
                    for half in range(2):
                        last = nc.tensor.transpose(MB[0:C, half * HALF:(half + 1) * HALF], on[:, half, :],
                                                   ident[0:HALF, 0:HALF])
                    last.then_inc(onT_ready, 1)
                row_max(t + 1, 4)
                row_max(t + 1, 5)
                logits(t, 2)
                if b.within(B):
                    pe.wait_ge(onT_out, b.n + 1)
                    for half in range(2):
                        last = mm(MB[0:HALF, half * C:(half + 1) * C], onT[:, half * HALF:(half + 1) * HALF], w_proj[:, :],
                                  start=True, stop=True)
                    last.then_inc(pr_ready, 1)
                row_max(t + 1, 6)
                b = t + 3
                if b.within(B):
                    if (b + 1).within(B):
                        pe.wait_ge(rank_done, TC * (b.n + 2))
                    held(pe, xn_done, 2 * (b.n + 1), spare)
                    for half in range(2):
                        last = nc.tensor.transpose(MA[0:C, half * HALF:(half + 1) * HALF], xn[:, half, :],
                                                   ident[0:HALF, 0:HALF])
                    last.then_inc(xnT_ready, 1)
                row_max(t + 1, 7)
                weigh(t, 0)
                weigh(t, 1)
                logits(t, 3)
                if b.within(B):
                    pe.wait_ge(xnT_out, b.n + 1)
                    for half in range(2):
                        last = mm(MA[0:HALF, half * 3 * C:(half + 1) * 3 * C], xnT[:, half * HALF:(half + 1) * HALF],
                                  w_qkv[:, :], start=True, stop=True)
                    last.then_inc(qkv_ready, 1)
                weigh(t, 2)

            pe.wait_ge(const_act, CONST_ACT)
            pe.wait_ge(const_dve, CONST_DVE)
            pe.wait_ge(c_qkvb, 16)
            pe.wait_ge(c_projb, 16)
            pe.wait_ge(bias_loaded, 16 * 6)
            steps(pe, step)

            pe.wait_ge(c_moe, 160)
            pe.wait_ge(h_done, B)
            nc.tensor.transpose(MB[:, 0:E], b1raw[:, :], ident[0:E, 0:E]).then_inc(const_pe, 1)
            pe.wait_ge(const_dve, CONST_DVE + 3)

            def first(c, e):
                if not c.within(NCH):
                    return
                if e == 0:
                    pe.wait_ge(xsT_out, c.n + 1)
                passed(pe, gelu_done, E * c.n + e - 1)
                for k in range(2):
                    at = 1024 * (e % 2) + 512 * k
                    for part in range(2):
                        last = mm(s2[:, at:at + 376], w1s[:, e, part, :], xsT[:, c.buf, 376 * k:376 * (k + 1)],
                                  start=part == 0, stop=part == 1)
                last.then_inc(h_ready, 1)

            def second(c, j):
                if not c.within(NCH):
                    return
                if j == 0:
                    pe.wait_ge(gelu_done, E * (c.n + 1))
                passed(pe, y_dve, 24 * c.n + 3 * (j - 2) + 1)
                o = s1[0:HALF, 512 * (j % 2):512 * (j % 2) + 512]
                for part in range(2):
                    mm(o, ones16[:, :], b2hl[:, part, :], start=part == 0, stop=part == 1)
                for e in range(E):
                    last = mm(o[:, e * C:(e + 1) * C], hT[:, c.buf, e, j * HALF:(j + 1) * HALF], w2[:, e, :],
                              start=False, stop=True, skip_group_check=True)
                last.then_inc(y_ready, 1)

            def chunk(c):
                for j in range(CT):
                    first(c + 1, j)
                    second(c, j)
                b = c + 2
                if b.within(NCH):
                    pe.wait_ge(n_pool, 31 * (b.n + 1))
                    passed(pe, gates, 16 * b.n)
                    for j in range(CT):
                        last = nc.tensor.transpose(MA16[:, j * HALF:(j + 1) * HALF], xs[:, j, :], ident16[0:HALF, 0:HALF])
                    last.then_inc(xsT_ready, 1)
                    pe.wait_ge(xsT_out, b.n + 1)
                    for j in range(CT):
                        for part in range(2):
                            last = mm(MA[0:HALF, j * E:(j + 1) * E], xsT[:, b.buf, j * HALF:(j + 1) * HALF],
                                      wrs[:, part, :], start=part == 0, stop=part == 1)
                    last.then_inc(lg_ready, 1)

            chunk_steps(pe, chunk)


LOG100 = 4.605170185988092
CONST_DVE = 7
CONST_ACT = 7 + 2 * H

_INS = ["x", "L0_tok_score_proj", "L0_attn_qkv_w", "L0_attn_qkv_b", "L0_attn_proj_w", "L0_attn_proj_b",
        "L0_attn_logit_scale", "L0_attn_mlp1_w", "L0_attn_mlp1_b", "L0_attn_mlp2_w", "L0_attn_mlp2_b",
        "L0_ffn_gamma", "L0_ffn_beta", "L0_ffn_Wr", "L0_ffn_br", "L0_ffn_W1", "L0_ffn_b1", "L0_ffn_W2",
        "L0_ffn_b2"]


def kernel(**inputs):
    import numpy as np
    import concourse.bacc as bacc
    from concourse.bass_utils import run_bass_kernel_spmd

    d = np.arange(REL) - (NSEL - 1)
    r = (np.sign(d) * np.log1p(np.abs(d).astype(np.float32))).astype(np.float32)
    rel_log = np.stack([np.zeros(2 * REL, np.float32), np.concatenate([r, r[::-1]])])

    nc = bacc.Bacc("TRN2", target_bir_lowering=False, num_devices=1)
    arrays, args = {}, []
    for name in _INS:
        a = np.ascontiguousarray(inputs[name])
        arrays[f"in_{name}_dram"] = a
        args.append(nc.dram_tensor(f"in_{name}_dram", a.shape, mybir.dt.from_np(a.dtype), kind="ExternalInput").ap())
    arrays["rel_log_dram"] = rel_log
    args.append(nc.dram_tensor("rel_log_dram", rel_log.shape, mybir.dt.float32, kind="ExternalInput").ap())
    args.append(nc.dram_tensor("out_dram", (B, NSEL, C), mybir.dt.float32, kind="ExternalOutput").ap())
    audio_tower(nc, *args)
    result = run_bass_kernel_spmd(nc, [arrays], core_ids=[0])
    return result.results[0]["out_dram"]
```

```python
import concourse.bass as bass
from concourse import mybir
from contextlib import ExitStack

B, N, C = 32, 375, 64
NSEL = N // 2
H, D = 8, 8
E, HID = 8, 128
META = 96
HALF = (NSEL + 1) // 2
LQ = 2 * HALF
REST = NSEL - HALF
TP, TC = 125, 3
REL = LQ + NSEL - 1
KSCALE = 16.0
WSCALE = 64.0
QW = 32
NCH, CB = 8, 4
CT = 2 * CB
EPS = 1e-5
MAGIC = float(0x5F3759DF)


class Batch:

    def __init__(self, pair, rest):
        self.pair, self.rest = pair, rest

    def __add__(self, d):
        return Batch(self.pair, self.rest + d)

    @property
    def n(self):
        return 2 * self.pair + self.rest

    @property
    def buf(self):
        return self.rest % 2

    @property
    def turn(self):
        return self.pair + self.rest // 2

    def within(self, count):
        return not isinstance(self.pair, int) or 0 <= self.n < count


def passed(eng, sem, value):
    if not isinstance(value, int) or value > 0:
        eng.wait_ge(sem, value)


def held(eng, sem, value, spare):
    passed(eng, sem, value)
    eng.sem_inc(spare, 1)


def audio_tower(nc, x, score_proj, qkv_w, qkv_b, proj_w, proj_b, logit_scale, mlp1_w, mlp1_b,
                mlp2_w, mlp2_b, gamma, beta, Wr, br, W1, b1, W2, b2, rel_log, out):
    f32, f16, i32 = mybir.dt.float32, mybir.dt.float16, mybir.dt.int32
    ALU, ACT, AX = mybir.AluOpType, mybir.ActivationFunctionType, mybir.AxisListType

    bias_dram = nc.dram_tensor("bias_scratch", (3, H, HALF, REL), f16, kind="Internal").ap()

    ctx = ExitStack()
    with ctx:
        def sb(name, shape, dt=f32):
            return ctx.enter_context(nc.sbuf_tensor(name, shape, dt))

        def ps(name, banks):
            return ctx.enter_context(nc.psum_tensor(name, [128, 512 * banks], f32))

        def sem(name):
            return ctx.enter_context(nc.semaphore(name))

        ident = sb("ident", [128, 128])
        ident16 = sb("ident16", [128, 128], f16)
        before = sb("before", [TP, TC, N])
        tiny = sb("tiny", [TP, N])
        place_i = sb("place_i", [TP, LQ], i32)
        place = sb("place", [TP, LQ])
        wscore = sb("wscore", [TP, C])
        w_qkv = sb("w_qkv", [C + 1, 3 * C])
        w_proj = sb("w_proj", [C + 1, C])
        w_raw = sb("w_raw", [META, 2, C])
        wp_raw = sb("wp_raw", [C, C])
        qk_scale = sb("qk_scale", [HALF, 2, 2, H])
        ls = sb("ls", [HALF, H])
        rel = sb("rel", [2, 2 * REL])
        m1t = sb("m1t", [2, META])
        m1b = sb("m1b", [META, 1])
        m2t = sb("m2t", [META, H])
        m2rep = sb("m2rep", [META, H, 128])
        m2b = sb("m2b", [128, H])
        m2bs = sb("m2bs", [128, H])
        hid = sb("hid", [META, 2 * REL])
        hT = sb("hT", [HID, 2, E, CT * HALF])
        hT_flat = hT[0:HALF, :, :, :].rearrange("p b e n -> p (b e n)")
        dist = hT_flat[:, 0:2 * H * REL].rearrange("p (r h w) -> p r h w", r=2, h=H)
        dist16 = hT_flat[:, 2 * H * REL:2 * H * REL + 3 * H * REL // 2].bitcast(f16).rearrange("p (r h w) -> p r h w", r=3, h=H)
        bias_q = sb("bias_q", [128, 2, H, NSEL], f16)
        bias_k = sb("bias_k", [128, 2, 2, H, LQ], f16)

        X = sb("X", [TP, 2, TC, C + 1])
        prod = sb("prod", [TP, TC, C])
        flags = sb("flags", [TP, TC, N], f16)
        rank = sb("rank", [TP, 2, TC])
        onehot = sb("onehot", [TP, 2, TC, LQ])
        sel = sb("sel", [HALF, 2, C + 1])
        egate = sb("egate", [HALF, 2])
        gate = sb("gate", [HALF, 2])
        stats = sb("stats", [HALF, 2, 6])
        mv = sb("mv", [HALF, 2, 2, 2])
        xn = sb("xn", [HALF, 2, C])
        xnT = sb("xnT", [C + 1, LQ])
        qkv = sb("qkv", [HALF, 2, 2, 3 * C])
        sq = sb("sq", [HALF, 2, 2 * C])
        nv = sb("nv", [HALF, 4 * H + 2])
        ni = sb("ni", [HALF, 4 * H + 2], i32)
        ny = sb("ny", [HALF, 4 * H + 2])
        nt = sb("nt", [HALF, 4 * H + 2])
        qk_factor = sb("qk_factor", [HALF, 4 * H])
        qn = sb("qn", [HALF, 2, 2 * C])
        stack = sb("stack", [HALF, 2, 2, 2, H, QW], f16)
        qT1 = sb("qT1", [128, 2, 2, LQ], f16)
        kT = sb("kT", [128, 2, 2, 4, LQ], f16)
        qT2 = sb("qT2", [128, 2, LQ], f16)
        V = sb("V", [128, 2, 2, H, QW])
        P = sb("P", [128, 4, 4, LQ])
        oT = sb("oT", [128, 2, LQ])
        rz = sb("rz", [HALF, 16])
        on = sb("on", [HALF, 2, C])
        onT = sb("onT", [C + 1, LQ])
        hsel = sb("hsel", [HALF, B, 2, C])

        w1raw = sb("w1raw", [128, E, HID])
        w1s = sb("w1s", [128, E, 2, HID], f16)
        w2 = sb("w2", [HID, E, C])
        b1c = sb("b1c", [HID, E])
        b1raw = sb("b1raw", [E, HID])
        b2raw = sb("b2raw", [1, E * C])
        b2hl = sb("b2hl", [1, 2, E * C], f16)
        ones16 = sb("ones16", [1, HALF], f16)
        wr_raw = sb("wr_raw", [128, E])
        wrs = sb("wrs", [128, 2, E], f16)
        br_b = sb("br_b", [HALF, E])
        gam = sb("gam", [HALF, C])
        bet = sb("bet", [HALF, C])
        prio_i = sb("prio_i", [HALF, E], i32)
        prio = sb("prio", [HALF, E])
        n_stats = sb("n_stats", [HALF, CT, 6])
        n_mv = sb("n_mv", [HALF, CT, 2])
        n_v = sb("n_v", [HALF, CT])
        n_i = sb("n_i", [HALF, CT], i32)
        n_y = sb("n_y", [HALF, CT])
        n_t = sb("n_t", [HALF, CT])
        n_x = sb("n_x", [HALF, CT, C])
        n_z = sb("n_z", [HALF, CT, C])
        xs = sb("xs", [HALF, CT, 2 * C], f16)
        xsT = sb("xsT", [128, 2, CT * HALF], f16)
        lg = sb("lg", [HALF, CT, E])
        lg2 = sb("lg2", [HALF, CT, E])
        eq = sb("eq", [HALF, CT, E])
        oh1 = sb("oh1", [HALF, CT, E])
        oh2 = sb("oh2", [HALF, CT, E])
        top1 = sb("top1", [HALF, CT])
        top2 = sb("top2", [HALF, CT])
        pick = sb("pick", [HALF, CT])
        dif = sb("dif", [HALF, CT])
        th = sb("th", [HALF, CT])
        wa = sb("wa", [HALF, CT])
        wb = sb("wb", [HALF, CT])
        wfull = sb("wfull", [HALF, 2, CT, E])
        yw = sb("yw", [HALF, 2, E, C])
        yr = sb("yr", [HALF, 2, C])
        yo = sb("yo", [HALF, 2, CT, C])

        s1 = ps("s1", 2)
        s2 = ps("s2", 4)
        MA = ps("MA", 1)
        MB = ps("MB", 1)
        MA16 = MA[:, :].bitcast(f16)
        MC = s2[:, 1024:1536]
        MT16 = s2[:, 1536:2048].bitcast(f16)
        t2_view = MT16[:, 0:2 * LQ].rearrange("p (g l) -> p g l", g=2)
        t1_view = MT16[:, 0:4 * LQ].rearrange("p (q g l) -> p q g l", q=2, g=2)

        names = """c_wscore c_qkvw c_qkvb c_projw c_projb c_ls c_rel c_mlp c_moe c_moeb const_pool const_dve const_act
            const_pe bias_stored bias_loaded score ranks_row rank_done onehot_done gathered sel_out
            gate_steps xn_done xnT_ready xnT_out qkv_ready qkv_out norm_steps newton_done
            stack_dve stack_hi max_clear t1_ready t1_out v_done s1_ready neg_max t2_ready t2_out
            s2_ready exp_done pv_done oT_out to_ready on_done onT_ready onT_out pr_ready h_done
            n_stat n_pool n_hi xsT_ready xsT_out lg_ready gates th_done h_ready gelu_done y_ready
            y_dve out_done0 out_done1""".split()
        S = {n: sem(n) for n in names}
        (c_wscore, c_qkvw, c_qkvb, c_projw, c_projb, c_ls, c_rel, c_mlp, c_moe, c_moeb, const_pool, const_dve, const_act,
         const_pe, bias_stored, bias_loaded, score, ranks_row, rank_done, onehot_done, gathered,
         sel_out, gate_steps, xn_done, xnT_ready, xnT_out, qkv_ready, qkv_out,
         norm_steps, newton_done, stack_dve, stack_hi, max_clear, t1_ready, t1_out, v_done,
         s1_ready, neg_max, t2_ready, t2_out, s2_ready, exp_done, pv_done, oT_out, to_ready,
         on_done, onT_ready, onT_out, pr_ready, h_done, n_stat, n_pool, n_hi, xsT_ready, xsT_out,
         lg_ready, gates, th_done, h_ready, gelu_done, y_ready, y_dve, out_done0,
         out_done1) = [S[n] for n in names]
        x_loaded = [sem("x_loaded0"), sem("x_loaded1")]
        spare = sem("spare")
        out_done = [out_done0, out_done1]

        x_v = x.rearrange("b (p c) f -> b p c f", c=TC)

        FIRST, LAST = 2, B - 6

        def steps(eng, step):
            for t in range(-5, FIRST):
                step(Batch(0, t))
            with eng.Fori(FIRST // 2, LAST // 2) as k:
                step(Batch(k, 0))
                step(Batch(k, 1))
            for t in range(LAST, B + 1):
                step(Batch(0, t))

        def chunk_steps(eng, step):
            for c in range(-2, 2):
                step(Batch(0, c))
            with eng.Fori(1, (NCH - 2) // 2) as k:
                step(Batch(k, 0))
                step(Batch(k, 1))
            for c in range(NCH - 2, NCH):
                step(Batch(0, c))

        block = ctx.enter_context(nc.Block())

        @block.sync
        def _(sp):
            def load_x(b):
                passed(sp, gathered, b.n - 1)
                sp.dma_start(X[:, b.buf, :, 0:C], x_v[b.n, :, :, :]).then_inc(x_loaded[b.buf], 16)

            sp.dma_start(wscore[:, :], score_proj.rearrange("f o -> o f").broadcast_to([TP, C])).then_inc(c_wscore, 16)
            load_x(Batch(0, 0))
            load_x(Batch(0, 1))
            for tile in range(2):
                for part in range(2):
                    src = bass.AP(bias_dram.tensor, bias_dram.offset + part * H * HALF * REL + NSEL - 1 - HALF * tile,
                                  [[REL - 1, HALF - tile], [HALF * REL, H], [1, LQ]])
                    if tile == 0 and part == 0:
                        sp.wait_ge(bias_stored, 16)
                    sp.dma_start(bias_k[0:HALF - tile, tile, part, :, :], src).then_inc(bias_loaded, 16)
                src = bass.AP(bias_dram.tensor, bias_dram.offset + 2 * H * HALF * REL + NSEL - HALF * tile,
                              [[REL - 1, HALF], [HALF * REL, H], [1, NSEL]])
                sp.dma_start(bias_q[0:HALF, tile, :, :], src).then_inc(bias_loaded, 16)

            with sp.Fori(1, B // 2) as k:
                load_x(Batch(k, 0))
                load_x(Batch(k, 1))

            def store(c):
                if not c.within(NCH):
                    return
                sp.wait_ge(y_dve, 24 * (c.n + 1))
                for half, rows in ((0, HALF), (1, REST)):
                    dst = out[bass.ds(c.n * CB, CB), half * HALF:half * HALF + rows, :].rearrange("b p f -> p b f")
                    src = yo[0:rows, c.buf, :, :].rearrange("p (b t) f -> p b t f", t=2)[:, :, half, :]
                    sp.dma_start(dst, src).then_inc(out_done[c.buf], 16)

            chunk_steps(sp, store)
            sp.wait_ge(out_done[0], 16 * NCH)
            sp.wait_ge(out_done[1], 16 * NCH)

        @block.gpsimd
        def _(pool):
            nc.gpsimd.memset(ident[:, :], 0.0).then_inc(const_pool, 1)
            nc.gpsimd.memset(tiny[:, :], -1e-37).then_inc(const_pool, 1)
            nc.gpsimd.iota(place_i[:, :], pattern=[[1, LQ]], base=0, channel_multiplier=0).then_inc(const_pool, 1)
            nc.gpsimd.iota(prio_i[:, :], pattern=[[-1, E]], base=E, channel_multiplier=0).then_inc(const_pool, 1)
            pool.wait_ge(const_pool, 4)
            nc.gpsimd.affine_select(out=ident[:, :], in_=ident[:, :], compare_op=ALU.not_equal, fill=1.0,
                                    base=0, pattern=[[-1, 128]], channel_multiplier=1).then_inc(const_pool, 1)
            for c in range(TC):
                nc.gpsimd.affine_select(out=before[:, c, :], in_=tiny[:, :], compare_op=ALU.is_gt, fill=0.0,
                                        base=c, pattern=[[-1, TC], [-3, TP]],
                                        channel_multiplier=TC).then_inc(const_pool, 1)

            def newton(sems, count, base, y, v, t):
                for r in range(3):
                    nc.gpsimd.tensor_tensor(t, y, y, ALU.mult).then_inc(sems, 1)
                    pool.wait_ge(sems, base + 4 * r + 1)
                    nc.gpsimd.tensor_tensor(t, t, v, ALU.mult).then_inc(sems, 1)
                    held(pool, sems, base + 4 * r + 2, spare)
                    nc.gpsimd.tensor_scalar(t, t, -0.5, 1.5, ALU.mult, ALU.add).then_inc(sems, 1)
                    pool.wait_ge(sems, base + 4 * r + 3)
                    nc.gpsimd.tensor_tensor(y, y, t, ALU.mult).then_inc(sems, 1)
                    if r < 2 or count > 12:
                        pool.wait_ge(sems, base + 4 * r + 4)

            def step(t):
                b = t + 1
                if b.within(B):
                    pool.wait_ge(qkv_out, 2 * (b.n + 1))
                    held(pool, pv_done, 4 * (b.n - 1), spare)
                    for tile in range(2):
                        nc.gpsimd.tensor_copy(V[0:HALF, b.buf, tile, :, 0:D],
                                              qkv[:, b.buf, tile, 2 * C:3 * C].rearrange("p (h d) -> p h d", d=D)
                                              ).then_inc(v_done, 1)
                b = t + 2
                if b.within(B):
                    held(pool, t2_ready, b.n - 1, spare)
                    nc.gpsimd.memset(stack[:, b.buf, :, 0, :, 24:25].rearrange("p t h o -> p t (h o)"),
                                     0.0).then_inc(max_clear, 1)
                b = t + 5
                if b.within(B):
                    pool.wait_ge(rank_done, TC * (b.n + 1))
                    held(pool, gathered, b.n - 1, spare)
                    for c in range(TC):
                        nc.gpsimd.tensor_scalar(onehot[:, b.buf, c, :], place[:, :], rank[:, b.buf, c:c + 1],
                                                None, ALU.is_equal).then_inc(onehot_done, 1)
                turn = t + 4
                if turn.within(B + 1):
                    pool.wait_ge(norm_steps, 5 * (turn.n + 1))
                    newton(newton_done, 13, 13 * turn.n, ny[:, :], nv[:, :], nt[:, :])
                    passed(pool, stack_dve, 3 * turn.n - 5)
                    nc.gpsimd.tensor_tensor(qk_factor[:, :], ny[:, 0:4 * H],
                                            qk_scale[:, :, :, :].rearrange("p t q h -> p (t q h)"),
                                            ALU.mult).then_inc(newton_done, 1)

            pool.wait_ge(const_dve, CONST_DVE)
            pool.wait_ge(const_act, CONST_ACT)
            steps(pool, step)

            def bc(v):
                return v.rearrange("p (t o) -> p t o", o=1).broadcast_to([HALF, CT, C])

            def rows(v):
                return v.rearrange("p (o f) -> p o f", o=1).broadcast_to([HALF, CT, C])

            def chunk(c):
                b = c + 2
                if not b.within(NCH):
                    return
                at = 31 * b.n
                h4 = hsel[:, bass.ds(b.n * CB, CB), :, :].rearrange("p b t f -> p (b t) f")
                for again in range(2):
                    pool.wait_ge(n_stat, 38 * b.n + 19 * (again + 1))
                    newton(n_pool, 13, at + 14 * again, n_y[:, :], n_v[:, :], n_t[:, :])
                    src = h4 if again == 0 else n_x[:, :, :]
                    nc.gpsimd.tensor_tensor(n_z[:, :, :], src, bc(n_mv[:, :, 0]), ALU.subtract).then_inc(n_pool, 1)
                    pool.wait_ge(n_pool, at + 14 * again + 13)
                    if again == 0:
                        nc.gpsimd.tensor_tensor(n_x[:, :, :], n_z[:, :, :], bc(n_y[:, :]), ALU.mult).then_inc(n_pool, 1)
                        pool.wait_ge(n_pool, at + 14)
                    else:
                        nc.gpsimd.tensor_tensor(n_z[:, :, :], n_z[:, :, :], bc(n_y[:, :]), ALU.mult).then_inc(n_pool, 1)
                        pool.wait_ge(n_pool, at + 28)
                nc.gpsimd.tensor_tensor(n_z[:, :, :], n_z[:, :, :], rows(gam[:, :]), ALU.mult).then_inc(n_pool, 1)
                pool.wait_ge(n_pool, at + 29)
                passed(pool, n_hi, b.n)
                nc.gpsimd.tensor_tensor(n_x[:, :, :], n_z[:, :, :], rows(bet[:, :]), ALU.add).then_inc(n_pool, 1)
                pool.wait_ge(n_pool, at + 30)
                pool.wait_ge(n_hi, b.n + 1)
                nc.gpsimd.tensor_tensor(xs[:, :, C:2 * C], n_x[:, :, :], xs[:, :, 0:C],
                                        ALU.subtract).then_inc(n_pool, 1)

            pool.wait_ge(h_done, B)
            chunk_steps(pool, chunk)

        @block.scalar
        def _(act):
            for half in range(2):
                act.dma_start(w_raw[:, half, :], qkv_w[half * META:(half + 1) * META, :]).then_inc(c_qkvw, 16)
            act.dma_start(w_qkv[C:C + 1, :], qkv_b.rearrange("(o n) -> o n", o=1)).then_inc(c_qkvb, 16)
            act.dma_start(wp_raw[:, :], proj_w).then_inc(c_projw, 16)
            act.dma_start(w_proj[C:C + 1, :], proj_b.rearrange("(o n) -> o n", o=1)).then_inc(c_projb, 16)
            act.dma_start(ls[:, :], logit_scale.rearrange("(o n) -> o n", o=1).broadcast_to([HALF, H])).then_inc(c_ls, 16)
            act.dma_start(rel[:, :], rel_log).then_inc(c_rel, 16)
            act.dma_start(m1t[:, :], mlp1_w.rearrange("m c -> c m"), allow_slow_non_contiguous=True).then_inc(c_mlp, 16)
            act.dma_start(m1b[:, :], mlp1_b.rearrange("(m o) -> m o", o=1)).then_inc(c_mlp, 16)
            act.dma_start(m2t[:, :], mlp2_w.rearrange("h m -> m h"), allow_slow_non_contiguous=True).then_inc(c_mlp, 16)
            act.dma_start(m2b[:, :], mlp2_b.rearrange("(o n) -> o n", o=1).broadcast_to([128, H])).then_inc(c_mlp, 16)
            act.wait_ge(c_mlp, 64)
            for r in range(2):
                act.wait_ge(const_pe, r + 1)
                nc.scalar.activation(hid[:, r * REL:(r + 1) * REL], s1[0:META, 512 * r:512 * r + REL], ACT.Relu,
                                     bias=m1b[:, :]).then_inc(const_act, 1)
            act.wait_ge(const_pe, 5)
            nc.scalar.activation(w_qkv[0:C, 0:META], MA[0:C, 0:META], ACT.Copy).then_inc(const_act, 1)
            nc.scalar.activation(w_qkv[0:C, META:2 * META], MA[0:C, META:2 * META], ACT.Copy).then_inc(const_act, 1)
            nc.scalar.activation(w_proj[0:C, :], MA[0:C, 192:192 + C], ACT.Copy).then_inc(const_act, 1)
            act.wait_ge(const_dve, 1)
            for half in range(2):
                nc.scalar.activation(qk_scale[:, half, 0, :], ls[:, :], ACT.Exp).then_inc(const_act, 1)
            act.wait_ge(const_dve, 2)
            for n in range(2 * H):
                r, h = n // H, n % H
                act.wait_ge(const_pe, 6 + n)
                nc.scalar.activation(dist[:, r, h, :], s2[0:HALF, 512 * (n % 4):512 * (n % 4) + REL], ACT.Identity,
                                     bias=m2bs[0:HALF, h:h + 1], scale=KSCALE).then_inc(const_act, 1)
            act.dma_start(w1raw[0:C, :, :], W1.rearrange("e d h -> d e h")).then_inc(c_moe, 16)
            act.dma_start(w1raw[C:2 * C, :, :], W1.rearrange("e d h -> d e h")).then_inc(c_moe, 16)
            act.dma_start(wr_raw[0:C, :], Wr).then_inc(c_moe, 16)
            act.dma_start(wr_raw[C:2 * C, :], Wr).then_inc(c_moe, 16)
            act.dma_start(w2[:, :, :], W2.rearrange("e h d -> h e d")).then_inc(c_moe, 16)
            act.dma_start(b1raw[:, :], b1).then_inc(c_moe, 16)
            act.dma_start(b2raw[:, :], b2.rearrange("(o e) d -> o (e d)", o=1)).then_inc(c_moe, 16)
            act.dma_start(br_b[:, :], br.rearrange("(o n) -> o n", o=1).broadcast_to([HALF, E])).then_inc(c_moe, 16)
            act.dma_start(gam[:, :], gamma.rearrange("(o n) -> o n", o=1).broadcast_to([HALF, C])).then_inc(c_moe, 16)
            act.dma_start(bet[:, :], beta.rearrange("(o n) -> o n", o=1).broadcast_to([HALF, C])).then_inc(c_moe, 16)
            act.wait_ge(const_dve, 5)
            act.dma_start(bias_dram.rearrange("r h p w -> p (r h) w"),
                          dist16.rearrange("p r h w -> p (r h) w")).then_inc(bias_stored, 16)

            def exps(b, pair):
                if not b.within(B):
                    return
                rows = HALF - pair % 2
                passed(act, pv_done, 4 * (b.n - 1) + pair + 1)
                for k in range(2):
                    act.wait_ge(s2_ready, 8 * b.n + 2 * pair + k + 1)
                    nc.scalar.activation(P[0:rows, pair, 2 * k:2 * k + 2, :].rearrange("p j l -> p (j l)"),
                                         s2[0:rows, 512 * k:512 * k + 2 * LQ], ACT.Exp,
                                         scale=1.0 / KSCALE).then_inc(exp_done, 1)

            def step(t):
                b = t + (-1)
                if b.within(B):
                    act.wait_ge(pv_done, 4 * (b.n + 1))
                    passed(act, to_ready, b.n)
                    nc.scalar.activation(oT[:, :, :], MB[:, 0:2 * LQ].rearrange("p (g l) -> p g l", g=2),
                                         ACT.Copy).then_inc(oT_out, 1)
                b = t
                if b.within(B):
                    act.wait_ge(t2_ready, b.n + 1)
                    passed(act, s2_ready, 8 * b.n)
                    nc.scalar.activation(qT2[:, :, :], t2_view,
                                         ACT.Copy).then_inc(t2_out, 1)
                b = t + 4
                if b.within(B):
                    act.wait_ge(gathered, b.n + 1)
                    passed(act, gate_steps, 7 * b.n)
                    nc.scalar.activation(sel[:, :, :], MA[0:HALF, 0:2 * (C + 1)].rearrange("p (t f) -> p t f", t=2),
                                         ACT.Copy).then_inc(sel_out, 1)
                    act.wait_ge(sel_out, 2 * b.n + 1)
                    nc.scalar.activation(egate[:, :], sel[:, :, C], ACT.Exp, scale=-1.0).then_inc(sel_out, 1)
                exps(t, 0)
                b = t + 3
                if b.within(B):
                    act.wait_ge(xnT_ready, b.n + 1)
                    passed(act, qkv_ready, b.n)
                    nc.scalar.activation(xnT[0:C, :], MC[0:C, 0:LQ], ACT.Copy).then_inc(xnT_out, 1)
                b = t + (-1)
                if b.within(B):
                    act.wait_ge(onT_ready, b.n + 1)
                    passed(act, pr_ready, b.n)
                    nc.scalar.activation(onT[0:C, :], MB[0:C, 0:LQ], ACT.Copy).then_inc(onT_out, 1)
                exps(t, 1)
                b = t + 3
                if b.within(B):
                    act.wait_ge(qkv_ready, b.n + 1)
                    passed(act, v_done, 2 * (b.n - 1))
                    passed(act, stack_dve, 3 * (b.n - 2) + 1)
                    pv = MC[0:HALF, 0:6 * C].rearrange("p (t f) -> p t f", t=2)
                    nc.scalar.activation(qkv[:, b.buf, :, :], pv, ACT.Copy).then_inc(qkv_out, 1)
                    passed(act, norm_steps, 5 * b.n + 1)
                    nc.scalar.activation(sq[:, :, :], pv[:, :, 0:2 * C], ACT.Square).then_inc(qkv_out, 1)
                exps(t, 2)
                b = t + 2
                if b.within(B):
                    act.wait_ge(stack_dve, 3 * b.n + 1)
                    passed(act, t2_ready, b.n - 1)
                    nc.scalar.activation(stack[:, b.buf, :, :, :, 0:D].rearrange("p t q h d -> p (t q h) d"),
                                         qn[:, :, :].rearrange("p t (g d) -> p (t g) d", d=D),
                                         ACT.Copy).then_inc(stack_hi, 1)
                    for qk, at in ((0, D), (1, 2 * D)):
                        nc.scalar.activation(stack[:, b.buf, :, qk, :, at:at + D],
                                             qn[:, :, qk * C:(qk + 1) * C].rearrange("p t (h d) -> p t h d", d=D),
                                             ACT.Copy).then_inc(stack_hi, 1)
                exps(t, 3)
                b = t + 2
                if b.within(B):
                    act.wait_ge(t1_ready, b.n + 1)
                    passed(act, s1_ready, 8 * (b.n - 1))
                    nc.scalar.activation(qT1[:, b.buf, :, :], t1_view[:, 0, :, :],
                                         ACT.Copy).then_inc(t1_out, 1)
                    passed(act, s2_ready, 8 * (b.n - 1))
                    for hh in range(4):
                        q = slice(32 * hh, 32 * hh + 32)
                        nc.scalar.activation(kT[q, b.buf, :, hh, :],
                                             t1_view[q, 1, :, :],
                                             ACT.Copy).then_inc(t1_out, 1)

            steps(act, step)

            act.wait_ge(const_pe, 22)
            nc.scalar.activation(b1c[:, :], MB[:, 0:E], ACT.Copy).then_inc(const_act, 1)
            act.wait_ge(const_act, CONST_ACT + 1)

            def chunk(c):
                b = c + 2
                layer = c + 1
                for e in range(E):
                    if layer.within(NCH):
                        act.wait_ge(h_ready, E * layer.n + e + 1)
                        if e == 0:
                            passed(act, y_ready, CT * (layer.n - 1))
                        hv = s2[:, 1024 * (e % 2):1024 * (e % 2) + 1024].rearrange("p (k c) -> p k c", k=2)[:, :, 0:376]
                        nc.scalar.activation(hT[:, layer.buf, e, :].rearrange("p (k c) -> p k c", k=2), hv, ACT.Gelu,
                                             bias=b1c[:, e:e + 1], scale=1.0 / WSCALE).then_inc(gelu_done, 1)
                    if e == 5 and b.within(NCH):
                        act.wait_ge(n_pool, 31 * b.n + 30)
                        passed(act, xsT_ready, b.n)
                        nc.scalar.activation(xs[:, :, 0:C], n_x[:, :, :], ACT.Copy).then_inc(n_hi, 1)
                if b.within(NCH):
                    act.wait_ge(xsT_ready, b.n + 1)
                    passed(act, h_ready, E * (b.n - 1))
                    passed(act, lg_ready, b.n - 1)
                    nc.scalar.activation(xsT[:, b.buf, :], MA16[:, 0:CT * HALF], ACT.Copy).then_inc(xsT_out, 1)
                    act.wait_ge(gates, 16 * b.n + 13)
                    nc.scalar.activation(th[:, :], dif[:, :], ACT.Tanh, scale=0.5).then_inc(th_done, 1)

            chunk_steps(act, chunk)

        @block.vector
        def _(dve):
            nc.vector.memset(bias_q[64:128, :, :, :], 0.0)
            nc.vector.memset(bias_k[64:128, :, :, :, :], 0.0)
            dve.wait_ge(c_ls, 16)
            nc.vector.tensor_scalar(ls[:, :], ls[:, :], LOG100, None, ALU.min).then_inc(const_dve, 1)
            dve.wait_ge(c_mlp, 64)
            nc.vector.tensor_scalar(m2bs[:, :], m2b[:, :], KSCALE, None, ALU.mult)
            nc.vector.tensor_copy(m2rep[:, :, :], m2t[:, :].rearrange("p (h o) -> p h o", o=1)
                                  .broadcast_to([META, H, 128])).then_inc(const_dve, 1)
            dve.wait_ge(const_act, 7 + 2 * H)
            nc.vector.tensor_copy(dist16[:, 0, :, :], dist[:, 0, :, :]).then_inc(const_dve, 1)
            nc.vector.tensor_copy(dist16[:, 2, :, :], dist[:, 1, :, :]).then_inc(const_dve, 1)
            dve.wait_ge(const_dve, 3)
            nc.vector.tensor_tensor(dist16[:, 1, :, :], dist[:, 0, :, :], dist16[:, 0, :, :],
                                    ALU.subtract).then_inc(const_dve, 1)
            dve.wait_ge(const_pool, 8)
            nc.vector.tensor_copy(ident16[:, :], ident[:, :])
            nc.vector.tensor_copy(place[:, :], place_i[:, :])
            nc.vector.tensor_copy(prio[:, :], prio_i[:, :])
            nc.vector.memset(qk_scale[:, :, 1, :], KSCALE)
            nc.vector.memset(xnT[C:C + 1, :], 1.0)
            nc.vector.memset(onT[C:C + 1, :], 1.0)
            nc.vector.memset(ones16[:, :], 1.0)
            nc.vector.memset(kT[:, :, :, :, :], 0.0)
            nc.vector.memset(V[:, :, :, :, :], 0.0)
            nc.vector.memset(P[:, :, :, :], 0.0)
            nc.vector.memset(nv[:, :], 1.0)
            nc.vector.memset(sq[:, :, :], 1.0)
            nc.vector.memset(stack[:, :, :, :, :, :], 0.0).then_inc(const_dve, 1)
            dve.wait_ge(const_dve, 6)
            nc.vector.memset(stack[:, :, :, 1, :, 24:25].rearrange("p b t h o -> p (b t) (h o)"), 1.0)
            nc.vector.memset(V[0:HALF, :, :, :, D:D + 1].rearrange("p b t h o -> p (b t) (h o)"), 1.0).then_inc(const_dve, 1)

            def split_max(b, n):
                if not b.within(B):
                    return
                half, j = n // 4, n % 4
                dve.wait_ge(s1_ready, 8 * b.n + n + 1)
                nc.vector.tensor_reduce(stack[:, b.buf, half, 0, 2 * j:2 * j + 2, 24:25],
                                        s1[0:HALF, 512 * (n % 2):512 * (n % 2) + 2 * NSEL].rearrange("p (h m) -> p h m", h=2),
                                        AX.X, ALU.max, negate=True).then_inc(neg_max, 1)

            def step(t):
                squares = sq[:, :, :].rearrange("p t (g d) -> p (t g) d", d=D)
                scored, gated, turn, normed, last = t + 5, t + 4, t + 3, t + 2, t + (-1)
                if (t + 5).within(B):
                    b = t + 5
                    dve.wait_ge(x_loaded[b.buf], 16 * (b.turn + 1))
                    passed(dve, score, 2 * b.n)
                    nc.vector.tensor_tensor(prod[:, :, :], X[:, b.buf, :, 0:C],
                                            wscore[:, :].rearrange("p (o f) -> p o f", o=1).broadcast_to([TP, TC, C]),
                                            ALU.mult).then_inc(score, 1)
                if (t + 5).within(B):
                    b = t + 5
                    dve.wait_ge(score, 2 * b.n + 1)
                    passed(dve, gathered, b.n - 1)
                    nc.vector.tensor_reduce(X[:, b.buf, :, C:C + 1], prod[:, :, :], AX.X, ALU.add).then_inc(score, 1)
                if last.within(B):
                    dve.wait_ge(to_ready, last.n + 1)
                    to = MB[0:HALF, :].rearrange("p (g w) -> p g w", w=QW)
                    nc.vector.reciprocal(rz[:, :].rearrange("p (g o) -> p g o", o=1), to[:, :, D:D + 1]).then_inc(on_done, 1)
                    dve.wait_ge(on_done, 2 * last.n + 1)
                    nc.vector.tensor_tensor(on[:, :, :].rearrange("p t (g d) -> p (t g) d", d=D), to[:, :, 0:D],
                                            rz[:, :].rearrange("p (g o) -> p g o", o=1).broadcast_to([HALF, 16, D]),
                                            ALU.mult).then_inc(on_done, 1)
                if turn.within(B):
                    b = turn
                    dve.wait_ge(newton_done, 13 * b.n + 12)
                    passed(dve, xnT_ready, b.n)
                    for half in range(2):
                        nc.vector.tensor_scalar(xn[:, half, :], hsel[:, bass.ds(b.n, 1), half, :].rearrange("p o f -> p (o f)"),
                                                mv[:, b.buf, half, 0:1], ny[:, 4 * H + half:4 * H + half + 1], ALU.subtract,
                                                ALU.mult).then_inc(xn_done, 1)
                if normed.within(B):
                    b = normed
                    dve.wait_ge(newton_done, 13 * (b.n + 2))
                    passed(dve, stack_hi, 3 * b.n)
                    nc.vector.tensor_tensor(qn[:, :, :].rearrange("p t (g d) -> p t g d", d=D),
                                            qkv[:, b.buf, :, 0:2 * C].rearrange("p t (g d) -> p t g d", d=D),
                                            qk_factor[:, :].rearrange("p (t g o) -> p t g o", t=2, o=1).broadcast_to([HALF, 2, 2 * H, D]),
                                            ALU.mult).then_inc(stack_dve, 1)
                if gated.within(B):
                    b, k = gated, 7 * gated.n
                    dve.wait_ge(sel_out, 2 * (b.n + 1))
                    nc.vector.tensor_scalar(egate[:, :], egate[:, :], 1.0, None, ALU.add).then_inc(gate_steps, 1)
                    dve.wait_ge(gate_steps, k + 1)
                    nc.vector.reciprocal(gate[:, :], egate[:, :]).then_inc(gate_steps, 1)
                    dve.wait_ge(gate_steps, k + 2)
                    hb = hsel[:, bass.ds(b.n, 1), :, :].rearrange("p o t f -> p (o t) f")
                    nc.vector.tensor_tensor(hb, sel[:, :, 0:C],
                                            gate[:, :].rearrange("p (t o) -> p t o", o=1).broadcast_to([HALF, 2, C]),
                                            ALU.mult).then_inc(gate_steps, 1)
                if scored.within(B):
                    b = scored
                    dve.wait_ge(ranks_row, b.n + 1)
                    passed(dve, onehot_done, TC * (b.n - 1))
                    passed(dve, rank_done, TC * b.n)
                    for c in range(TC):
                        nc.vector.scalar_tensor_tensor(flags[:, c, :], MA[0:TP, 0:N], X[:, b.buf, c, C:C + 1],
                                                       before[:, c, :], ALU.subtract, ALU.is_gt,
                                                       accum_out=rank[:, b.buf, c:c + 1]).then_inc(rank_done, 1)
                if gated.within(B):
                    b, k = gated, 7 * gated.n
                    held(dve, gate_steps, k + 3, spare)
                    for half in range(2):
                        nc.vector.bn_stats(stats[:, half, :], hsel[:, bass.ds(b.n, 1), half, :].rearrange("p o f -> p (o f)")
                                           ).then_inc(gate_steps, 1)
                if last.within(B):
                    dve.wait_ge(pr_ready, last.n + 1)
                    hb = hsel[:, bass.ds(last.n, 1), :, :].rearrange("p o t f -> p (o t f)")
                    nc.vector.tensor_tensor(hb, hb, MB[0:HALF, 0:2 * C], ALU.add).then_inc(h_done, 1)
                split_max(t + 1, 0)
                if gated.within(B):
                    held(dve, gate_steps, k + 5, spare)
                    for half in range(2):
                        nc.vector.bn_aggr(mv[:, gated.buf, half, :], stats[:, half, :]).then_inc(gate_steps, 1)
                split_max(t + 1, 1)
                if (t + 4).within(B + 1):
                    b, p = t + 4, 5 * (t + 4).n
                    passed(dve, qkv_out, 2 * b.n)
                    passed(dve, newton_done, 13 * b.n)
                    nc.vector.tensor_reduce(nv[:, 0:4 * H].rearrange("p (g o) -> p g o", o=1), squares, AX.X,
                                            ALU.add).then_inc(norm_steps, 1)
                if (t + 4).within(B + 1):
                    b = t + 4
                    passed(dve, gate_steps, 7 * (b.n + 1) if b.within(B) else 7 * B)
                    nc.vector.tensor_scalar(nv[:, 4 * H:4 * H + 2], mv[:, b.buf, :, 1], EPS, None,
                                            ALU.add).then_inc(norm_steps, 1)
                if (t + 4).within(B + 1):
                    dve.wait_ge(norm_steps, p + 1)
                    nc.vector.tensor_scalar(nv[:, 0:4 * H], nv[:, 0:4 * H], 1e-24, None, ALU.max).then_inc(norm_steps, 1)
                split_max(t + 1, 2)
                if (t + 4).within(B + 1):
                    dve.wait_ge(norm_steps, p + 3)
                    nc.vector.tensor_scalar(ni[:, :], nv[:, :].bitcast(i32), 1, None,
                                            ALU.logical_shift_right).then_inc(norm_steps, 1)
                if normed.within(B):
                    b = normed
                    dve.wait_ge(stack_hi, 3 * b.n + 1)
                    for qk, at in ((0, 2 * D), (1, D)):
                        nc.vector.tensor_tensor(stack[:, b.buf, :, qk, :, at:at + D],
                                                qn[:, :, qk * C:(qk + 1) * C].rearrange("p t (h d) -> p t h d", d=D),
                                                stack[:, b.buf, :, qk, :, 0:D], ALU.subtract).then_inc(stack_dve, 1)
                if (t + 4).within(B + 1):
                    dve.wait_ge(norm_steps, p + 4)
                    nc.vector.tensor_scalar(ny[:, :].bitcast(i32), ni[:, :], -1.0, MAGIC, ALU.mult,
                                            ALU.add).then_inc(norm_steps, 1)
                split_max(t + 1, 3)
                split_max(t + 1, 4)
                split_max(t + 1, 5)
                split_max(t + 1, 6)
                split_max(t + 1, 7)

            dve.wait_ge(c_wscore, 16)
            steps(dve, step)

            dve.wait_ge(c_moe, 160)
            nc.vector.tensor_scalar(w1raw[:, :, :], w1raw[:, :, :], WSCALE, None, ALU.mult)
            nc.vector.tensor_scalar(wr_raw[:, :], wr_raw[:, :], WSCALE, None, ALU.mult).then_inc(const_dve, 1)
            dve.wait_ge(const_dve, CONST_DVE + 1)
            nc.vector.tensor_copy(w1s[:, :, 0, :], w1raw[:, :, :])
            nc.vector.tensor_copy(wrs[:, 0, :], wr_raw[:, :])
            nc.vector.tensor_copy(b2hl[:, 0, :], b2raw[:, :]).then_inc(const_dve, 1)
            dve.wait_ge(const_dve, CONST_DVE + 2)
            nc.vector.tensor_tensor(w1s[:, :, 1, :], w1raw[:, :, :], w1s[:, :, 0, :], ALU.subtract)
            nc.vector.tensor_tensor(wrs[:, 1, :], wr_raw[:, :], wrs[:, 0, :], ALU.subtract)
            nc.vector.tensor_tensor(b2hl[:, 1, :], b2raw[:, :], b2hl[:, 0, :], ALU.subtract).then_inc(const_dve, 1)
            dve.wait_ge(h_done, B)

            def guess(b, again):
                k = 38 * b.n + 19 * again
                src = (hsel[:, bass.ds(b.n * CB, CB), :, :].rearrange("p b t f -> p (b t) f")
                       if again == 0 else n_x[:, :, :])
                for j in range(CT):
                    nc.vector.bn_stats(n_stats[:, j, :], src[:, j, :]).then_inc(n_stat, 1)
                held(dve, n_stat, k + 8, spare)
                for j in range(CT):
                    nc.vector.bn_aggr(n_mv[:, j, :], n_stats[:, j, :]).then_inc(n_stat, 1)
                dve.wait_ge(n_stat, k + 16)
                nc.vector.tensor_scalar(n_v[:, :], n_mv[:, :, 1], EPS, None, ALU.add).then_inc(n_stat, 1)
                dve.wait_ge(n_stat, k + 17)
                nc.vector.tensor_scalar(n_i[:, :], n_v[:, :].bitcast(i32), 1, None,
                                        ALU.logical_shift_right).then_inc(n_stat, 1)
                dve.wait_ge(n_stat, k + 18)
                nc.vector.tensor_scalar(n_y[:, :].bitcast(i32), n_i[:, :], -1.0, MAGIC, ALU.mult,
                                        ALU.add).then_inc(n_stat, 1)

            def combine(c, j):
                if not c.within(NCH):
                    return
                k = 24 * c.n + 3 * j
                if j == 0:
                    dve.wait_ge(gates, 16 * (c.n + 1))
                dve.wait_ge(y_ready, CT * c.n + j + 1)
                nc.vector.tensor_tensor(yw[:, j % 2, :, :],
                                        s1[0:HALF, 512 * (j % 2):512 * (j % 2) + 512].rearrange("p (e d) -> p e d", e=E),
                                        wfull[:, c.buf, j, :].rearrange("p (e o) -> p e o", o=1).broadcast_to([HALF, E, C]),
                                        ALU.mult).then_inc(y_dve, 1)
                dve.wait_ge(y_dve, k + 1)
                nc.vector.tensor_reduce(yr[:, j % 2, :].rearrange("p (d o) -> p d o", o=1),
                                        yw[:, j % 2, :, :].rearrange("p e d -> p d e"), AX.X, ALU.add).then_inc(y_dve, 1)
                dve.wait_ge(y_dve, k + 2)
                hb = hsel[:, bass.ds(c.n * CB + j // 2, 1), j % 2, :].rearrange("p o f -> p (o f)")
                nc.vector.tensor_tensor(yo[:, c.buf, j, :], yr[:, j % 2, :], hb, ALU.add).then_inc(y_dve, 1)

            def b8(v):
                return v.rearrange("p (t o) -> p t o", o=1).broadcast_to([HALF, CT, E])

            def over_e(v):
                return v.rearrange("p (o e) -> p o e", o=1).broadcast_to([HALF, CT, E])

            def chunk(c):
                b = c + 2
                if b.within(NCH):
                    held(dve, n_pool, 31 * b.n, spare)
                    guess(b, 0)
                if c.within(NCH):
                    passed(dve, out_done[c.buf], 32 * c.turn)
                for j in range(3):
                    combine(c, j)
                if b.within(NCH):
                    held(dve, n_pool, 31 * b.n + 14, spare)
                    guess(b, 1)
                for j in range(3, 8):
                    combine(c, j)
                if b.within(NCH):
                    k = 16 * b.n
                    dve.wait_ge(lg_ready, b.n + 1)
                    nc.vector.scalar_tensor_tensor(lg[:, :, :], MA[0:HALF, 0:CT * E].rearrange("p (t e) -> p t e", e=E),
                                                   1.0 / WSCALE, over_e(br_b[:, :]), ALU.mult, ALU.add).then_inc(gates, 1)
                    for r, (src, top, oh) in enumerate(((lg, top1, oh1), (lg2, top2, oh2))):
                        k += 6 * r
                        dve.wait_ge(gates, k + 1)
                        nc.vector.tensor_reduce(top[:, :].rearrange("p (t o) -> p t o", o=1), src[:, :, :], AX.X,
                                                ALU.max).then_inc(gates, 1)
                        dve.wait_ge(gates, k + 2)
                        nc.vector.tensor_tensor(eq[:, :, :], src[:, :, :], b8(top[:, :]), ALU.is_equal).then_inc(gates, 1)
                        dve.wait_ge(gates, k + 3)
                        nc.vector.tensor_tensor(eq[:, :, :], eq[:, :, :], over_e(prio[:, :]), ALU.mult).then_inc(gates, 1)
                        dve.wait_ge(gates, k + 4)
                        nc.vector.tensor_reduce(pick[:, :].rearrange("p (t o) -> p t o", o=1), eq[:, :, :], AX.X,
                                                ALU.max).then_inc(gates, 1)
                        dve.wait_ge(gates, k + 5)
                        nc.vector.tensor_tensor(oh[:, :, :], eq[:, :, :], b8(pick[:, :]), ALU.is_equal).then_inc(gates, 1)
                        dve.wait_ge(gates, k + 6)
                        if r == 0:
                            nc.vector.scalar_tensor_tensor(lg2[:, :, :], oh1[:, :, :], -1e30, lg[:, :, :], ALU.mult,
                                                           ALU.add).then_inc(gates, 1)
                    nc.vector.tensor_tensor(dif[:, :], top1[:, :], top2[:, :], ALU.subtract).then_inc(gates, 1)
                    k = 16 * b.n + 13
                    dve.wait_ge(th_done, b.n + 1)
                    nc.vector.tensor_scalar(wa[:, :], th[:, :], 0.5, 0.5, ALU.mult, ALU.add)
                    nc.vector.tensor_scalar(wb[:, :], th[:, :], -0.5, 0.5, ALU.mult, ALU.add).then_inc(gates, 1)
                    dve.wait_ge(gates, k + 1)
                    nc.vector.tensor_tensor(oh1[:, :, :], oh1[:, :, :], b8(wa[:, :]), ALU.mult)
                    nc.vector.tensor_tensor(oh2[:, :, :], oh2[:, :, :], b8(wb[:, :]), ALU.mult).then_inc(gates, 1)
                    dve.wait_ge(gates, k + 2)
                    nc.vector.tensor_tensor(wfull[:, b.buf, :, :], oh1[:, :, :], oh2[:, :, :], ALU.add).then_inc(gates, 1)

            chunk_steps(dve, chunk)

        @block.tensor
        def _(pe):
            mm = nc.tensor.matmul
            pe.wait_ge(c_rel, 16)
            pe.wait_ge(c_mlp, 64)
            for r in range(2):
                mm(s1[0:META, 512 * r:512 * r + REL], m1t[:, :], rel[:, r * REL:(r + 1) * REL], start=True,
                   stop=True).then_inc(const_pe, 1)
            pe.wait_ge(const_pool, 5)
            pe.wait_ge(c_qkvw, 32)
            pe.wait_ge(c_projw, 16)
            for r in range(2):
                nc.tensor.transpose(MA[0:C, r * META:(r + 1) * META], w_raw[:, r, :], ident[0:META, 0:META]).then_inc(const_pe, 1)
            nc.tensor.transpose(MA[0:C, 192:192 + C], wp_raw[:, :], ident[0:C, 0:C]).then_inc(const_pe, 1)
            pe.wait_ge(const_act, 2)
            pe.wait_ge(const_dve, 2)
            for n in range(2 * H):
                r, h = n // H, n % H
                if n >= 4:
                    pe.wait_ge(const_act, 7 + n - 3)
                mm(s2[:, 512 * (n % 4):512 * (n % 4) + REL], m2rep[:, h, :], hid[:, r * REL:(r + 1) * REL], start=True,
                   stop=True).then_inc(const_pe, 1)

            def row_max(b, n):
                if not b.within(B):
                    return
                half, j = n // 4, n % 4
                g, hh = j // 2, 2 * (j % 2)
                if n < 2:
                    pe.wait_ge(t1_out, 5 * b.n + 3 + 2 * n)
                passed(pe, neg_max, 8 * b.n + n - 1)
                o = s1[0:HALF, 512 * (n % 2):512 * (n % 2) + 2 * NSEL]
                mm(o, ident16[:, 0:HALF], bias_q[:, half, 2 * j:2 * j + 2, :].rearrange("p h m -> p (h m)"),
                   start=True, stop=False)
                mm(o.rearrange("p (h m) -> p h m", h=2), qT1[:, b.buf, g, half * HALF:(half + 1) * HALF],
                   kT[:, b.buf, g, hh:hh + 2, 0:NSEL], start=False, stop=True).then_inc(s1_ready, 1)

            def logits(b, u):
                if not b.within(B):
                    return
                g, tile, k = u // 4, u // 2 % 2, u % 2
                rows = HALF - tile
                if u == 0:
                    pe.wait_ge(t2_out, b.n + 1)
                passed(pe, exp_done, 8 * b.n + u - 1)
                at, h0 = 512 * k, 4 * g + 2 * k
                for part in range(2):
                    mm(s2[0:rows, at:at + 2 * LQ], ident16[:, 0:rows],
                       bias_k[:, tile, part, h0:h0 + 2, :].rearrange("p h l -> p (h l)"),
                       start=part == 0, stop=part == 1)
                for j in range(2):
                    last = mm(s2[0:rows, at + j * LQ:at + (j + 1) * LQ],
                              kT[:, b.buf, g, 2 * k + j, tile * HALF:tile * HALF + rows], qT2[:, g, :],
                              start=False, stop=True, skip_group_check=True)
                last.then_inc(s2_ready, 1)

            def weigh(b, u):
                if not b.within(B):
                    return
                g, tile = u // 2, u % 2
                pe.wait_ge(exp_done, 8 * b.n + 2 * u + 2)
                if u == 0:
                    pe.wait_ge(v_done, 2 * (b.n + 1))
                    passed(pe, h_done, b.n)
                for hh in range(4):
                    last = mm(MB[32 * hh:32 * hh + QW, g * LQ:(g + 1) * LQ], V[:, b.buf, tile, 4 * g + hh, :],
                              P[:, u, hh, :], start=tile == 0, stop=tile == 1, tile_position=(0, 32 * hh),
                              skip_group_check=True)
                last.then_inc(pv_done, 1)

            def step(t):
                b = t + 4
                if b.within(B):
                    pe.wait_ge(onehot_done, TC * (b.n + 1))
                    for half in range(2):
                        for c in range(TC):
                            last = mm(MA[0:HALF, half * (C + 1):(half + 1) * (C + 1)],
                                      onehot[:, b.buf, c, half * HALF:(half + 1) * HALF], X[:, b.buf, c, :],
                                      start=c == 0, stop=c == TC - 1)
                    last.then_inc(gathered, 1)
                b = t
                if b.within(B):
                    pe.wait_ge(neg_max, 8 * (b.n + 1))
                    pe.wait_ge(t1_out, 5 * min(b.n + 2, B) if isinstance(b.pair, int) else 5 * (b.n + 2))
                    for g in range(2):
                        for half in range(2):
                            last = nc.tensor.transpose(t2_view[:, g, half * HALF:(half + 1) * HALF],
                                                       stack[:, b.buf, half, 0, 4 * g:4 * g + 4, :].rearrange("p h w -> p (h w)"),
                                                       ident16[0:HALF, 0:HALF])
                    last.then_inc(t2_ready, 1)
                b = t + (-1)
                if b.within(B):
                    pe.wait_ge(oT_out, b.n + 1)
                    for half in range(2):
                        for g in range(2):
                            last = nc.tensor.transpose(MB[0:HALF, (2 * half + g) * 128:(2 * half + g + 1) * 128],
                                                       oT[:, g, half * HALF:(half + 1) * HALF], ident[:, :])
                    last.then_inc(to_ready, 1)
                logits(t, 0)
                b = t + 3
                if b.within(B):
                    passed(pe, qkv_out, 2 * b.n)
                    held(pe, xn_done, 2 * (b.n + 1), spare)
                    for half in range(2):
                        last = nc.tensor.transpose(MC[0:C, half * HALF:(half + 1) * HALF], xn[:, half, :],
                                                   ident[0:HALF, 0:HALF])
                    last.then_inc(xnT_ready, 1)
                b = t + 5
                if b.within(B):
                    pe.wait_ge(score, 2 * (b.n + 1))
                    passed(pe, sel_out, 2 * b.n - 1)
                    for c in range(TC):
                        last = nc.tensor.transpose(MA[0:TP, c * TP:(c + 1) * TP],
                                                   X[:, b.buf, c, C:C + 1].broadcast_to([TP, TP]), ident[0:TP, 0:TP])
                    last.then_inc(ranks_row, 1)
                logits(t, 1)
                b = t + (-1)
                if b.within(B):
                    held(pe, on_done, 2 * (b.n + 1), spare)
                    for half in range(2):
                        last = nc.tensor.transpose(MB[0:C, half * HALF:(half + 1) * HALF], on[:, half, :],
                                                   ident[0:HALF, 0:HALF])
                    last.then_inc(onT_ready, 1)
                logits(t, 2)
                b = t + 3
                if b.within(B):
                    pe.wait_ge(xnT_out, b.n + 1)
                    for half in range(2):
                        last = mm(MC[0:HALF, half * 3 * C:(half + 1) * 3 * C], xnT[:, half * HALF:(half + 1) * HALF],
                                  w_qkv[:, :], start=True, stop=True)
                    last.then_inc(qkv_ready, 1)
                logits(t, 3)
                b = t + (-1)
                if b.within(B):
                    pe.wait_ge(onT_out, b.n + 1)
                    for half in range(2):
                        last = mm(MB[0:HALF, half * C:(half + 1) * C], onT[:, half * HALF:(half + 1) * HALF], w_proj[:, :],
                                  start=True, stop=True)
                    last.then_inc(pr_ready, 1)
                row_max(t + 1, 0)
                logits(t, 4)
                row_max(t + 1, 1)
                logits(t, 5)
                row_max(t + 1, 2)
                logits(t, 6)
                row_max(t + 1, 3)
                logits(t, 7)
                row_max(t + 1, 4)
                b = t + 2
                if b.within(B):
                    pe.wait_ge(stack_dve, 3 * (b.n + 1))
                    pe.wait_ge(stack_hi, 3 * (b.n + 1))
                    pe.wait_ge(max_clear, b.n + 1)
                    passed(pe, t2_out, b.n - 1)
                    for qk in range(2):
                        for g in range(2):
                            for half in range(2):
                                last = nc.tensor.transpose(t1_view[:, qk, g, half * HALF:(half + 1) * HALF],
                                                           stack[:, b.buf, half, qk, 4 * g:4 * g + 4, :].rearrange("p h w -> p (h w)"),
                                                           ident16[0:HALF, 0:HALF])
                    last.then_inc(t1_ready, 1)
                weigh(t, 0)
                row_max(t + 1, 5)
                weigh(t, 1)
                row_max(t + 1, 6)
                weigh(t, 2)
                row_max(t + 1, 7)
                weigh(t, 3)

            pe.wait_ge(const_act, CONST_ACT)
            pe.wait_ge(const_dve, CONST_DVE)
            pe.wait_ge(c_qkvb, 16)
            pe.wait_ge(c_projb, 16)
            pe.wait_ge(bias_loaded, 16 * 6)
            steps(pe, step)

            pe.wait_ge(c_moe, 160)
            pe.wait_ge(h_done, B)
            nc.tensor.transpose(MB[:, 0:E], b1raw[:, :], ident[0:E, 0:E]).then_inc(const_pe, 1)
            pe.wait_ge(const_dve, CONST_DVE + 3)

            def first(c, e):
                if not c.within(NCH):
                    return
                if e == 0:
                    pe.wait_ge(xsT_out, c.n + 1)
                passed(pe, gelu_done, E * c.n + e - 1)
                for k in range(2):
                    at = 1024 * (e % 2) + 512 * k
                    for part in range(2):
                        last = mm(s2[:, at:at + 376], w1s[:, e, part, :], xsT[:, c.buf, 376 * k:376 * (k + 1)],
                                  start=part == 0, stop=part == 1)
                last.then_inc(h_ready, 1)

            def second(c, j):
                if not c.within(NCH):
                    return
                if j == 0:
                    pe.wait_ge(gelu_done, E * (c.n + 1))
                passed(pe, y_dve, 24 * c.n + 3 * (j - 2) + 1)
                o = s1[0:HALF, 512 * (j % 2):512 * (j % 2) + 512]
                for part in range(2):
                    mm(o, ones16[:, :], b2hl[:, part, :], start=part == 0, stop=part == 1)
                for e in range(E):
                    last = mm(o[:, e * C:(e + 1) * C], hT[:, c.buf, e, j * HALF:(j + 1) * HALF], w2[:, e, :],
                              start=False, stop=True, skip_group_check=True)
                last.then_inc(y_ready, 1)

            def chunk(c):
                for j in range(CT):
                    first(c + 1, j)
                    second(c, j)
                b = c + 2
                if b.within(NCH):
                    pe.wait_ge(n_pool, 31 * (b.n + 1))
                    passed(pe, gates, 16 * b.n)
                    for j in range(CT):
                        last = nc.tensor.transpose(MA16[:, j * HALF:(j + 1) * HALF], xs[:, j, :], ident16[0:HALF, 0:HALF])
                    last.then_inc(xsT_ready, 1)
                    pe.wait_ge(xsT_out, b.n + 1)
                    for j in range(CT):
                        for part in range(2):
                            last = mm(MA[0:HALF, j * E:(j + 1) * E], xsT[:, b.buf, j * HALF:(j + 1) * HALF],
                                      wrs[:, part, :], start=part == 0, stop=part == 1)
                    last.then_inc(lg_ready, 1)

            chunk_steps(pe, chunk)


LOG100 = 4.605170185988092
CONST_DVE = 7
CONST_ACT = 7 + 2 * H

_INS = ["x", "L0_tok_score_proj", "L0_attn_qkv_w", "L0_attn_qkv_b", "L0_attn_proj_w", "L0_attn_proj_b",
        "L0_attn_logit_scale", "L0_attn_mlp1_w", "L0_attn_mlp1_b", "L0_attn_mlp2_w", "L0_attn_mlp2_b",
        "L0_ffn_gamma", "L0_ffn_beta", "L0_ffn_Wr", "L0_ffn_br", "L0_ffn_W1", "L0_ffn_b1", "L0_ffn_W2",
        "L0_ffn_b2"]


def kernel(**inputs):
    import numpy as np
    import concourse.bacc as bacc
    from concourse.bass_utils import run_bass_kernel_spmd

    d = np.arange(REL) - (NSEL - 1)
    r = (np.sign(d) * np.log1p(np.abs(d).astype(np.float32))).astype(np.float32)
    rel_log = np.stack([np.zeros(2 * REL, np.float32), np.concatenate([r, r[::-1]])])

    nc = bacc.Bacc("TRN2", target_bir_lowering=False, num_devices=1)
    arrays, args = {}, []
    for name in _INS:
        a = np.ascontiguousarray(inputs[name])
        arrays[f"in_{name}_dram"] = a
        args.append(nc.dram_tensor(f"in_{name}_dram", a.shape, mybir.dt.from_np(a.dtype), kind="ExternalInput").ap())
    arrays["rel_log_dram"] = rel_log
    args.append(nc.dram_tensor("rel_log_dram", rel_log.shape, mybir.dt.float32, kind="ExternalInput").ap())
    args.append(nc.dram_tensor("out_dram", (B, NSEL, C), mybir.dt.float32, kind="ExternalOutput").ap())
    audio_tower(nc, *args)
    result = run_bass_kernel_spmd(nc, [arrays], core_ids=[0])
    return result.results[0]["out_dram"]
```

```python
import concourse.bass as bass
from concourse import mybir
from contextlib import ExitStack

B, N, C = 32, 375, 64
NSEL = N // 2
H, D = 8, 8
E, HID = 8, 128
META = 96
HALF = (NSEL + 1) // 2
LQ = 2 * HALF
REST = NSEL - HALF
TP, TC = 125, 3
REL = LQ + NSEL - 1
KSCALE = 16.0
WSCALE = 64.0
QW = 32
NCH, CB = 8, 4
CT = 2 * CB
EPS = 1e-5
MAGIC = float(0x5F3759DF)


class Batch:

    def __init__(self, pair, rest):
        self.pair, self.rest = pair, rest

    def __add__(self, d):
        return Batch(self.pair, self.rest + d)

    @property
    def n(self):
        return 2 * self.pair + self.rest

    @property
    def buf(self):
        return self.rest % 2

    @property
    def turn(self):
        return self.pair + self.rest // 2

    def within(self, count):
        return not isinstance(self.pair, int) or 0 <= self.n < count


def passed(eng, sem, value):
    if not isinstance(value, int) or value > 0:
        eng.wait_ge(sem, value)


def held(eng, sem, value, spare):
    passed(eng, sem, value)
    eng.sem_inc(spare, 1)


def audio_tower(nc, x, score_proj, qkv_w, qkv_b, proj_w, proj_b, logit_scale, mlp1_w, mlp1_b,
                mlp2_w, mlp2_b, gamma, beta, Wr, br, W1, b1, W2, b2, rel_log, out):
    f32, f16, i32 = mybir.dt.float32, mybir.dt.float16, mybir.dt.int32
    ALU, ACT, AX = mybir.AluOpType, mybir.ActivationFunctionType, mybir.AxisListType

    bias_dram = nc.dram_tensor("bias_scratch", (3, H, HALF, REL), f16, kind="Internal").ap()

    ctx = ExitStack()
    with ctx:
        def sb(name, shape, dt=f32):
            return ctx.enter_context(nc.sbuf_tensor(name, shape, dt))

        def ps(name, banks):
            return ctx.enter_context(nc.psum_tensor(name, [128, 512 * banks], f32))

        def sem(name):
            return ctx.enter_context(nc.semaphore(name))

        ident = sb("ident", [128, 128])
        ident16 = sb("ident16", [128, 128], f16)
        before = sb("before", [TP, TC, N])
        tiny = sb("tiny", [TP, N])
        place_i = sb("place_i", [TP, LQ], i32)
        place = sb("place", [TP, LQ])
        wscore = sb("wscore", [TP, C])
        w_qkv = sb("w_qkv", [C + 1, 3 * C])
        w_proj = sb("w_proj", [C + 1, C])
        w_raw = sb("w_raw", [META, 2, C])
        wp_raw = sb("wp_raw", [C, C])
        qk_scale = sb("qk_scale", [HALF, 2, 2, H])
        ls = sb("ls", [HALF, H])
        rel = sb("rel", [2, 2 * REL])
        m1t = sb("m1t", [2, META])
        m1b = sb("m1b", [META, 1])
        m2t = sb("m2t", [META, H])
        m2rep = sb("m2rep", [META, H, 128])
        m2b = sb("m2b", [128, H])
        m2bs = sb("m2bs", [128, H])
        hid = sb("hid", [META, 2 * REL])
        hT = sb("hT", [HID, 2, E, CT * HALF])
        hT_flat = hT[0:HALF, :, :, :].rearrange("p b e n -> p (b e n)")
        dist = hT_flat[:, 0:H * REL].rearrange("p (h w) -> p h w", h=H)
        dist16 = hT_flat[:, H * REL:H * REL + 3 * H * REL // 2].bitcast(f16).rearrange("p (r h w) -> p r h w", r=3, h=H)
        bias_q = sb("bias_q", [128, 2, H, NSEL], f16)
        bias_k = sb("bias_k", [128, 2, 2, H, LQ], f16)

        X = sb("X", [TP, 2, TC, C + 1])
        prod = sb("prod", [TP, TC, C])
        flags = sb("flags", [TP, TC, N], f16)
        rank = sb("rank", [TP, 2, TC])
        onehot = sb("onehot", [TP, 2, TC, LQ])
        sel = sb("sel", [HALF, 2, C + 1])
        egate = sb("egate", [HALF, 2])
        gate = sb("gate", [HALF, 2])
        stats = sb("stats", [HALF, 2, 6])
        mv = sb("mv", [HALF, 2, 2, 2])
        xn = sb("xn", [HALF, 2, C])
        xnT = sb("xnT", [C + 1, LQ])
        qkv = sb("qkv", [HALF, 2, 2, 3 * C])
        sq = sb("sq", [HALF, 2, 2 * C])
        nv = sb("nv", [HALF, 4 * H + 2])
        ni = sb("ni", [HALF, 4 * H + 2], i32)
        ny = sb("ny", [HALF, 4 * H + 2])
        nt = sb("nt", [HALF, 4 * H + 2])
        qk_factor = sb("qk_factor", [HALF, 4 * H])
        qn = sb("qn", [HALF, 2, 2 * C])
        stack = sb("stack", [HALF, 2, 2, 2, H, QW], f16)
        qT1 = sb("qT1", [128, 2, 2, LQ], f16)
        kT = sb("kT", [128, 2, 2, 4, LQ], f16)
        qT2 = sb("qT2", [128, 2, LQ], f16)
        V = sb("V", [128, 2, 2, H, QW])
        P = sb("P", [128, 4, 4, LQ])
        oT = sb("oT", [128, 2, LQ])
        rz = sb("rz", [HALF, 16])
        on = sb("on", [HALF, 2, C])
        onT = sb("onT", [C + 1, LQ])
        hsel = sb("hsel", [HALF, B, 2, C])

        w1raw = sb("w1raw", [128, E, HID])
        w1s = sb("w1s", [128, E, 2, HID], f16)
        w2 = sb("w2", [HID, E, C])
        b1c = sb("b1c", [HID, E])
        b1raw = sb("b1raw", [E, HID])
        b2raw = sb("b2raw", [2, E * C])
        b2hl = sb("b2hl", [2, 2, E * C], f16)
        b2rows = sb("b2rows", [128, E * C], f16)
        ones16 = sb("ones16", [128, HALF], f16)
        wr_raw = sb("wr_raw", [128, E])
        wrs = sb("wrs", [128, 2, E], f16)
        br_b = sb("br_b", [HALF, E])
        gam = sb("gam", [HALF, C])
        bet = sb("bet", [HALF, C])
        prio_i = sb("prio_i", [HALF, E], i32)
        prio = sb("prio", [HALF, E])
        n_stats = sb("n_stats", [HALF, CT, 6])
        n_mv = sb("n_mv", [HALF, CT, 2])
        n_v = sb("n_v", [HALF, CT])
        n_i = sb("n_i", [HALF, CT], i32)
        n_y = sb("n_y", [HALF, CT])
        n_t = sb("n_t", [HALF, CT])
        n_x = sb("n_x", [HALF, CT, C])
        n_z = sb("n_z", [HALF, CT, C])
        xs = sb("xs", [HALF, CT, 2 * C], f16)
        xsT = sb("xsT", [128, 2, CT * HALF], f16)
        lg = sb("lg", [HALF, CT, E])
        lg2 = sb("lg2", [HALF, CT, E])
        eq = sb("eq", [HALF, CT, E])
        oh1 = sb("oh1", [HALF, CT, E])
        oh2 = sb("oh2", [HALF, CT, E])
        top1 = sb("top1", [HALF, CT])
        top2 = sb("top2", [HALF, CT])
        pick = sb("pick", [HALF, CT])
        dif = sb("dif", [HALF, CT])
        th = sb("th", [HALF, CT])
        wa = sb("wa", [HALF, CT])
        wb = sb("wb", [HALF, CT])
        wfull = sb("wfull", [HALF, 2, CT, E])
        yw = sb("yw", [HALF, 2, E, C])
        yr = sb("yr", [HALF, 2, CT, C])
        yo = sb("yo", [HALF, 2, CT, C])

        s1 = ps("s1", 2)
        s2 = ps("s2", 4)
        MA = ps("MA", 1)
        MB = ps("MB", 1)
        MA16 = MA[:, :].bitcast(f16)
        MC = s2[:, 1024:1536]
        MT16 = s2[:, 1536:2048].bitcast(f16)
        t2_view = MT16[:, 0:2 * LQ].rearrange("p (g l) -> p g l", g=2)
        t1_view = MT16[:, 0:4 * LQ].rearrange("p (q g l) -> p q g l", q=2, g=2)

        names = """c_wscore c_qkvw c_qkvb c_projw c_projb c_ls c_rel c_mlp c_moe const_pool const_dve const_act
            const_pe bias_stored bias_loaded score ranks_row rank_done onehot_done gathered sel_out
            gate_steps xn_done xnT_ready xnT_out qkv_ready qkv_out norm_steps newton_done
            stack_dve stack_hi max_clear t1_ready t1_out v_done s1_ready neg_max t2_ready t2_out
            s2_ready exp_done pv_done oT_out to_ready on_done onT_ready onT_out pr_ready h_done
            n_stat n_pool n_hi xsT_ready xsT_out lg_ready gates th_done h_ready gelu_done y_ready
            y_read y_sum y_out out_done0 out_done1""".split()
        S = {n: sem(n) for n in names}
        (c_wscore, c_qkvw, c_qkvb, c_projw, c_projb, c_ls, c_rel, c_mlp, c_moe, const_pool, const_dve, const_act,
         const_pe, bias_stored, bias_loaded, score, ranks_row, rank_done, onehot_done, gathered,
         sel_out, gate_steps, xn_done, xnT_ready, xnT_out, qkv_ready, qkv_out,
         norm_steps, newton_done, stack_dve, stack_hi, max_clear, t1_ready, t1_out, v_done,
         s1_ready, neg_max, t2_ready, t2_out, s2_ready, exp_done, pv_done, oT_out, to_ready,
         on_done, onT_ready, onT_out, pr_ready, h_done, n_stat, n_pool, n_hi, xsT_ready, xsT_out,
         lg_ready, gates, th_done, h_ready, gelu_done, y_ready, y_read, y_sum, y_out, out_done0,
         out_done1) = [S[n] for n in names]
        x_loaded = [sem("x_loaded0"), sem("x_loaded1")]
        spare = sem("spare")
        out_done = [out_done0, out_done1]

        x_v = x.rearrange("b (p c) f -> b p c f", c=TC)

        FIRST, LAST = 2, B - 6

        def distance_bank(n):
            bank = 512 * (n % 2)
            return (s2 if n % 4 < 2 else s1)[:, bank:bank + REL]

        def steps(eng, step, after=()):
            for t in range(-5, FIRST):
                step(Batch(0, t))
                for at, work in after:
                    if t == at:
                        work()
            with eng.Fori(FIRST // 2, LAST // 2) as k:
                step(Batch(k, 0))
                step(Batch(k, 1))
            for t in range(LAST, B + 1):
                step(Batch(0, t))
                for at, work in after:
                    if t == at:
                        work()

        def chunk_steps(eng, step):
            for c in range(-1, 2):
                step(Batch(0, c))
            with eng.Fori(1, (NCH - 2) // 2) as k:
                step(Batch(k, 0))
                step(Batch(k, 1))
            for c in range(NCH - 2, NCH):
                step(Batch(0, c))

        block = ctx.enter_context(nc.Block())

        @block.sync
        def _(sp):
            def load_x(b):
                passed(sp, gathered, b.n - 1)
                sp.dma_start(X[:, b.buf, :, 0:C], x_v[b.n, :, :, :]).then_inc(x_loaded[b.buf], 16)

            sp.dma_start(wscore[:, :], score_proj.rearrange("f o -> o f").broadcast_to([TP, C])).then_inc(c_wscore, 16)
            load_x(Batch(0, 0))
            load_x(Batch(0, 1))
            load_x(Batch(0, 2))
            load_x(Batch(0, 3))
            for tile in range(2):
                for part in range(2):
                    src = bass.AP(bias_dram.tensor, bias_dram.offset + part * H * HALF * REL + NSEL - 1 - HALF * tile,
                                  [[REL - 1, HALF - tile], [HALF * REL, H], [1, LQ]])
                    if tile == 0 and part == 0:
                        sp.wait_ge(const_pool, 11)
                        sp.wait_ge(bias_stored, 16)
                    sp.dma_start(bias_k[0:HALF - tile, tile, part, :, :], src).then_inc(bias_loaded, 16)
                src = bass.AP(bias_dram.tensor, bias_dram.offset + 2 * H * HALF * REL + NSEL - HALF * tile,
                              [[REL - 1, HALF], [HALF * REL, H], [1, NSEL]])
                sp.dma_start(bias_q[0:HALF, tile, :, :], src).then_inc(bias_loaded, 16)
                load_x(Batch(0, 4 + tile))

            sp.dma_start(w1raw[0:C, :, :], W1.rearrange("e d h -> d e h")).then_inc(c_moe, 16)
            sp.dma_start(w1raw[C:2 * C, :, :], W1.rearrange("e d h -> d e h")).then_inc(c_moe, 16)
            sp.dma_start(wr_raw[0:C, :], Wr).then_inc(c_moe, 16)
            sp.dma_start(wr_raw[C:2 * C, :], Wr).then_inc(c_moe, 16)
            sp.dma_start(w2[:, :, :], W2.rearrange("e h d -> h e d")).then_inc(c_moe, 16)
            sp.dma_start(b1raw[:, :], b1).then_inc(c_moe, 16)
            for row in range(2):
                sp.dma_start(b2raw[row:row + 1, :], b2.rearrange("(o e) d -> o (e d)", o=1)).then_inc(c_moe, 16)
            sp.dma_start(br_b[:, :], br.rearrange("(o n) -> o n", o=1).broadcast_to([HALF, E])).then_inc(c_moe, 16)
            sp.dma_start(gam[:, :], gamma.rearrange("(o n) -> o n", o=1).broadcast_to([HALF, C])).then_inc(c_moe, 16)
            sp.dma_start(bet[:, :], beta.rearrange("(o n) -> o n", o=1).broadcast_to([HALF, C])).then_inc(c_moe, 16)

            with sp.Fori(3, B // 2) as k:
                load_x(Batch(k, 0))
                load_x(Batch(k, 1))

            def store(c):
                if not c.within(NCH):
                    return
                sp.wait_ge(y_out, c.n + 1)
                for half, rows in ((0, HALF), (1, REST)):
                    dst = out[bass.ds(c.n * CB, CB), half * HALF:half * HALF + rows, :].rearrange("b p f -> p b f")
                    src = yo[0:rows, c.buf, :, :].rearrange("p (b t) f -> p b t f", t=2)[:, :, half, :]
                    sp.dma_start(dst, src).then_inc(out_done[c.buf], 16)

            chunk_steps(sp, store)
            sp.wait_ge(out_done[0], 16 * NCH)
            sp.wait_ge(out_done[1], 16 * NCH)

        @block.gpsimd
        def _(pool):
            nc.gpsimd.memset(ident[:, :], 0.0).then_inc(const_pool, 1)
            nc.gpsimd.memset(tiny[:, :], -1e-37).then_inc(const_pool, 1)
            nc.gpsimd.iota(place_i[:, :], pattern=[[1, LQ]], base=0, channel_multiplier=0).then_inc(const_pool, 1)
            nc.gpsimd.iota(prio_i[:, :], pattern=[[-1, E]], base=E, channel_multiplier=0).then_inc(const_pool, 1)
            pool.wait_ge(const_pool, 4)
            nc.gpsimd.affine_select(out=ident[:, :], in_=ident[:, :], compare_op=ALU.not_equal, fill=1.0,
                                    base=0, pattern=[[-1, 128]], channel_multiplier=1).then_inc(const_pool, 1)
            for c in range(TC):
                nc.gpsimd.affine_select(out=before[:, c, :], in_=tiny[:, :], compare_op=ALU.is_gt, fill=0.0,
                                        base=c, pattern=[[-1, TC], [-3, TP]],
                                        channel_multiplier=TC).then_inc(const_pool, 1)

            def newton(sems, base, y, v, t):
                for r in range(3):
                    nc.gpsimd.tensor_tensor(t, y, y, ALU.mult).then_inc(sems, 1)
                    pool.wait_ge(sems, base + 4 * r + 1)
                    nc.gpsimd.tensor_tensor(t, t, v, ALU.mult).then_inc(sems, 1)
                    held(pool, sems, base + 4 * r + 2, spare)
                    nc.gpsimd.tensor_scalar(t, t, -0.5, 1.5, ALU.mult, ALU.add).then_inc(sems, 1)
                    pool.wait_ge(sems, base + 4 * r + 3)
                    nc.gpsimd.tensor_tensor(y, y, t, ALU.mult).then_inc(sems, 1)
                    pool.wait_ge(sems, base + 4 * r + 4)

            def step(t):
                b = t + 1
                if b.within(B):
                    pool.wait_ge(qkv_out, 2 * (b.n + 1))
                    held(pool, pv_done, 4 * (b.n - 1), spare)
                    for tile in range(2):
                        nc.gpsimd.tensor_copy(V[0:HALF, b.buf, tile, :, 0:D],
                                              qkv[:, b.buf, tile, 2 * C:3 * C].rearrange("p (h d) -> p h d", d=D)
                                              ).then_inc(v_done, 1)
                b = t + 2
                if b.within(B):
                    held(pool, t2_ready, b.n - 1, spare)
                    nc.gpsimd.memset(stack[:, b.buf, :, 0, :, 24:25].rearrange("p t h o -> p t (h o)"),
                                     0.0).then_inc(max_clear, 1)
                b = t + 5
                if b.within(B):
                    pool.wait_ge(rank_done, TC * (b.n + 1))
                    held(pool, gathered, b.n - 1, spare)
                    for c in range(TC):
                        nc.gpsimd.tensor_scalar(onehot[:, b.buf, c, :], place[:, :], rank[:, b.buf, c:c + 1],
                                                None, ALU.is_equal).then_inc(onehot_done, 1)
                turn = t + 4
                if turn.within(B + 1):
                    pool.wait_ge(norm_steps, 5 * (turn.n + 1))
                    newton(newton_done, 13 * turn.n, ny[:, :], nv[:, :], nt[:, :])
                    passed(pool, stack_dve, 3 * turn.n - 5)
                    nc.gpsimd.tensor_tensor(qk_factor[:, :], ny[:, 0:4 * H],
                                            qk_scale[:, :, :, :].rearrange("p t q h -> p (t q h)"),
                                            ALU.mult).then_inc(newton_done, 1)

            def pads():
                pool.wait_ge(onehot_done, TC)
                for n, pad in enumerate((bias_q[64:128, :, :, :],
                                         bias_k[64:128, :, :, :, :].bitcast(f32),
                                         P[64:128, :, :, :])):
                    pool.wait_ge(const_pool, 8 + n)
                    nc.gpsimd.memset(pad, 0.0).then_inc(const_pool, 1)
                pool.wait_ge(const_pool, 11)
                pool.wait_ge(const_act, 7)
                pool.wait_ge(const_dve, 6)

            pool.wait_ge(const_dve, 2)
            steps(pool, step, after=((-5, pads),))

            def rows(v):
                return v.rearrange("p (o f) -> p o f", o=1).broadcast_to([HALF, CT, C])

            def bc(v):
                return v.rearrange("p (t o) -> p t o", o=1).broadcast_to([HALF, CT, C])

            def norm(b):
                if not b.within(NCH):
                    return
                at = 17 * b.n
                h4 = hsel[:, bass.ds(b.n * CB, CB), :, :].rearrange("p b t f -> p (b t) f")
                pool.wait_ge(n_stat, 19 * (b.n + 1))
                newton(n_pool, at, n_y[:, :], n_v[:, :], n_t[:, :])
                nc.gpsimd.tensor_tensor(n_z[:, :, :], h4, bc(n_mv[:, :, 0]), ALU.subtract).then_inc(n_pool, 1)
                pool.wait_ge(n_pool, at + 13)
                nc.gpsimd.tensor_tensor(n_z[:, :, :], n_z[:, :, :], bc(n_y[:, :]), ALU.mult).then_inc(n_pool, 1)
                pool.wait_ge(n_pool, at + 14)
                nc.gpsimd.tensor_tensor(n_z[:, :, :], n_z[:, :, :], rows(gam[:, :]), ALU.mult).then_inc(n_pool, 1)
                pool.wait_ge(n_pool, at + 15)
                nc.gpsimd.tensor_tensor(n_x[:, :, :], n_z[:, :, :], rows(bet[:, :]), ALU.add).then_inc(n_pool, 1)
                pool.wait_ge(n_hi, b.n + 1)
                nc.gpsimd.tensor_tensor(xs[:, :, C:2 * C], n_x[:, :, :], xs[:, :, 0:C],
                                        ALU.subtract).then_inc(n_pool, 1)

            def residual(c):
                if not c.within(NCH):
                    return
                passed(pool, out_done[c.buf], 32 * c.turn)
                held(pool, y_sum, CT * (c.n + 1), spare)
                h4 = hsel[:, bass.ds(c.n * CB, CB), :, :].rearrange("p b t f -> p (b t) f")
                nc.gpsimd.tensor_tensor(yo[:, c.buf, :, :], yr[:, c.buf, :, :], h4, ALU.add).then_inc(y_out, 1)

            def chunk(c):
                norm(c + 2)
                residual(c)

            norm(Batch(0, 0))
            chunk_steps(pool, chunk)

        @block.scalar
        def _(act):
            act.dma_start(rel[:, :], rel_log).then_inc(c_rel, 16)
            act.dma_start(m1t[:, :], mlp1_w.rearrange("m c -> c m"), allow_slow_non_contiguous=True).then_inc(c_mlp, 16)
            act.dma_start(m1b[:, :], mlp1_b.rearrange("(m o) -> m o", o=1)).then_inc(c_mlp, 16)
            act.dma_start(m2t[:, :], mlp2_w.rearrange("h m -> m h"), allow_slow_non_contiguous=True).then_inc(c_mlp, 16)
            act.dma_start(m2b[:, :], mlp2_b.rearrange("(o n) -> o n", o=1).broadcast_to([128, H])).then_inc(c_mlp, 16)
            for half in range(2):
                act.dma_start(w_raw[:, half, :], qkv_w[half * META:(half + 1) * META, :]).then_inc(c_qkvw, 16)
            act.dma_start(w_qkv[C:C + 1, :], qkv_b.rearrange("(o n) -> o n", o=1)).then_inc(c_qkvb, 16)
            act.dma_start(wp_raw[:, :], proj_w).then_inc(c_projw, 16)
            act.dma_start(w_proj[C:C + 1, :], proj_b.rearrange("(o n) -> o n", o=1)).then_inc(c_projb, 16)
            act.dma_start(ls[:, :], logit_scale.rearrange("(o n) -> o n", o=1).broadcast_to([HALF, H])).then_inc(c_ls, 16)
            def distances():
                act.wait_ge(const_dve, 4)
                for n in range(2 * H):
                    r, h = n // H, n % H
                    act.wait_ge(const_pe, 6 + n)
                    nc.scalar.activation(dist[:, h, :] if r == 0 else dist16[:, 2, h, :],
                                         distance_bank(n)[0:HALF, :], ACT.Identity,
                                         bias=m2bs[0:HALF, h:h + 1], scale=KSCALE).then_inc(const_act, 1)
                act.wait_ge(const_dve, CONST_DVE)
                act.wait_ge(const_act, CONST_ACT)
                act.dma_start(bias_dram.rearrange("r h p w -> p (r h) w"),
                              dist16.rearrange("p r h w -> p (r h) w")).then_inc(bias_stored, 16)

            def hidden_layer():
                act.wait_ge(c_mlp, 64)
                for r in range(2):
                    act.wait_ge(const_pe, r + 1)
                    nc.scalar.activation(hid[:, r * REL:(r + 1) * REL], s1[0:META, 512 * r:512 * r + REL], ACT.Relu,
                                         bias=m1b[:, :]).then_inc(const_act, 1)
                act.wait_ge(const_pe, 5)
                nc.scalar.activation(w_qkv[0:C, 0:META], MB[0:C, 0:META], ACT.Copy).then_inc(const_act, 1)
                nc.scalar.activation(w_qkv[0:C, META:2 * META], MB[0:C, META:2 * META], ACT.Copy).then_inc(const_act, 1)
                nc.scalar.activation(w_proj[0:C, :], MB[0:C, 192:192 + C], ACT.Copy).then_inc(const_act, 1)
                act.wait_ge(const_dve, 3)
                for half in range(2):
                    nc.scalar.activation(qk_scale[:, half, 0, :], ls[:, :], ACT.Exp).then_inc(const_act, 1)

            def exps(b, pair):
                if not b.within(B):
                    return
                rows = HALF - pair % 2
                if isinstance(b.pair, int) and b.n == 0 and pair == 0:
                    act.wait_ge(const_pool, 11)
                passed(act, pv_done, 4 * (b.n - 1) + pair + 1)
                for k in range(2):
                    act.wait_ge(s2_ready, 8 * b.n + 2 * pair + k + 1)
                    nc.scalar.activation(P[0:rows, pair, 2 * k:2 * k + 2, :].rearrange("p j l -> p (j l)"),
                                         s2[0:rows, 512 * k:512 * k + 2 * LQ], ACT.Exp,
                                         scale=1.0 / KSCALE).then_inc(exp_done, 1)

            def step(t):
                b = t + (-1)
                if b.within(B):
                    act.wait_ge(pv_done, 4 * (b.n + 1))
                    passed(act, to_ready, b.n)
                    nc.scalar.activation(oT[:, :, :], MB[:, 0:2 * LQ].rearrange("p (g l) -> p g l", g=2),
                                         ACT.Copy).then_inc(oT_out, 1)
                b = t
                if b.within(B):
                    act.wait_ge(t2_ready, b.n + 1)
                    passed(act, s2_ready, 8 * b.n)
                    nc.scalar.activation(qT2[:, :, :], t2_view,
                                         ACT.Copy).then_inc(t2_out, 1)
                b = t + 4
                if b.within(B):
                    act.wait_ge(gathered, b.n + 1)
                    passed(act, gate_steps, 7 * b.n)
                    nc.scalar.activation(sel[:, :, :], MA[0:HALF, 0:2 * (C + 1)].rearrange("p (t f) -> p t f", t=2),
                                         ACT.Copy).then_inc(sel_out, 1)
                    act.wait_ge(sel_out, 2 * b.n + 1)
                    nc.scalar.activation(egate[:, :], sel[:, :, C], ACT.Exp, scale=-1.0).then_inc(sel_out, 1)
                exps(t, 0)
                b = t + 3
                if b.within(B):
                    act.wait_ge(xnT_ready, b.n + 1)
                    passed(act, qkv_ready, b.n)
                    nc.scalar.activation(xnT[0:C, :], MC[0:C, 0:LQ], ACT.Copy).then_inc(xnT_out, 1)
                b = t + (-1)
                if b.within(B):
                    act.wait_ge(onT_ready, b.n + 1)
                    passed(act, pr_ready, b.n)
                    nc.scalar.activation(onT[0:C, :], MB[0:C, 0:LQ], ACT.Copy).then_inc(onT_out, 1)
                exps(t, 1)
                b = t + 3
                if b.within(B):
                    act.wait_ge(qkv_ready, b.n + 1)
                    passed(act, v_done, 2 * (b.n - 1))
                    passed(act, stack_dve, 3 * (b.n - 2) + 1)
                    pv = MC[0:HALF, 0:6 * C].rearrange("p (t f) -> p t f", t=2)
                    nc.scalar.activation(qkv[:, b.buf, :, :], pv, ACT.Copy).then_inc(qkv_out, 1)
                    passed(act, norm_steps, 5 * b.n + 1)
                    nc.scalar.activation(sq[:, :, :], pv[:, :, 0:2 * C], ACT.Square).then_inc(qkv_out, 1)
                exps(t, 2)
                b = t + 2
                if b.within(B):
                    act.wait_ge(stack_dve, 3 * b.n + 1)
                    passed(act, t2_ready, b.n - 1)
                    nc.scalar.activation(stack[:, b.buf, :, :, :, 0:D].rearrange("p t q h d -> p (t q h) d"),
                                         qn[:, :, :].rearrange("p t (g d) -> p (t g) d", d=D),
                                         ACT.Copy).then_inc(stack_hi, 1)
                    for qk, at in ((0, D), (1, 2 * D)):
                        nc.scalar.activation(stack[:, b.buf, :, qk, :, at:at + D],
                                             qn[:, :, qk * C:(qk + 1) * C].rearrange("p t (h d) -> p t h d", d=D),
                                             ACT.Copy).then_inc(stack_hi, 1)
                exps(t, 3)
                b = t + 2
                if b.within(B):
                    act.wait_ge(t1_ready, b.n + 1)
                    passed(act, s1_ready, 8 * (b.n - 1))
                    nc.scalar.activation(qT1[:, b.buf, :, :], t1_view[:, 0, :, :],
                                         ACT.Copy).then_inc(t1_out, 1)
                    passed(act, s2_ready, 8 * (b.n - 1))
                    for hh in range(4):
                        q = slice(32 * hh, 32 * hh + 32)
                        nc.scalar.activation(kT[q, b.buf, :, hh, :],
                                             t1_view[q, 1, :, :],
                                             ACT.Copy).then_inc(t1_out, 1)

            def round_normed(b):
                act.wait_ge(n_pool, 17 * b.n + 16)
                passed(act, xsT_ready, b.n)
                nc.scalar.activation(xs[:, :, 0:C], n_x[:, :, :], ACT.Copy).then_inc(n_hi, 1)

            def copy_normed(b):
                act.wait_ge(xsT_ready, b.n + 1)
                passed(act, h_ready, E * (b.n - 1))
                passed(act, lg_ready, b.n - 1)
                nc.scalar.activation(xsT[:, b.buf, :], MA16[:, 0:CT * HALF], ACT.Copy).then_inc(xsT_out, 1)

            steps(act, step, after=((-5, hidden_layer), (-4, distances),
                                    (B - 1, lambda: round_normed(Batch(0, 0))),
                                    (B, lambda: copy_normed(Batch(0, 0)))))

            act.wait_ge(const_pe, 22)
            nc.scalar.activation(b1c[:, :], MB[:, 0:E], ACT.Copy).then_inc(const_act, 1)
            act.wait_ge(const_act, CONST_ACT + 1)

            def chunk(c):
                b = c + 2
                layer = c + 1
                for e in range(E):
                    if layer.within(NCH):
                        act.wait_ge(h_ready, E * layer.n + e + 1)
                        if e == 0:
                            passed(act, y_ready, CT * (layer.n - 1))
                        hv = s2[:, 1024 * (e % 2):1024 * (e % 2) + 1024].rearrange("p (k c) -> p k c", k=2)[:, :, 0:376]
                        nc.scalar.activation(hT[:, layer.buf, e, :].rearrange("p (k c) -> p k c", k=2), hv, ACT.Gelu,
                                             bias=b1c[:, e:e + 1], scale=1.0 / WSCALE).then_inc(gelu_done, 1)
                    if e == 4 and b.within(NCH):
                        round_normed(b)
                    if e == 6 and b.within(NCH):
                        copy_normed(b)
                    if e == 6 and layer.within(NCH):
                        act.wait_ge(gates, 16 * layer.n + 13)
                        nc.scalar.activation(th[:, :], dif[:, :], ACT.Tanh, scale=0.5).then_inc(th_done, 1)

            chunk_steps(act, chunk)

        @block.vector
        def _(dve):
            nc.vector.memset(qk_scale[:, :, 1, :], KSCALE)
            nc.vector.memset(xnT[C:C + 1, :], 1.0)
            nc.vector.memset(onT[C:C + 1, :], 1.0)
            nc.vector.memset(ones16[:, :], 1.0)
            nc.vector.memset(nv[:, :], 1.0)
            nc.vector.memset(sq[:, :, :], 1.0).then_inc(const_dve, 1)
            dve.wait_ge(const_pool, 8)
            nc.vector.tensor_copy(ident16[:, :], ident[:, :])
            nc.vector.tensor_copy(place[:, :], place_i[:, :])
            nc.vector.tensor_copy(prio[:, :], prio_i[:, :]).then_inc(const_dve, 1)
            def rest_of_setup():
                dve.wait_ge(c_ls, 16)
                nc.vector.tensor_scalar(ls[:, :], ls[:, :], LOG100, None, ALU.min).then_inc(const_dve, 1)
                dve.wait_ge(c_mlp, 64)
                nc.vector.tensor_scalar(m2bs[:, :], m2b[:, :], KSCALE, None, ALU.mult)
                nc.vector.tensor_copy(m2rep[:, :, :], m2t[:, :].rearrange("p (h o) -> p h o", o=1)
                                      .broadcast_to([META, H, 128])).then_inc(const_dve, 1)
                nc.vector.memset(b2rows[:, :], 0.0)
                nc.vector.memset(kT[:, :, :, :, :], 0.0)
                nc.vector.memset(V[:, :, :, :, :], 0.0)
                nc.vector.memset(stack[:, :, :, :, :, :], 0.0).then_inc(const_dve, 1)
                dve.wait_ge(const_dve, 5)
                nc.vector.memset(stack[:, :, :, 1, :, 24:25].rearrange("p b t h o -> p (b t) (h o)"), 1.0)
                nc.vector.memset(V[0:HALF, :, :, :, D:D + 1].rearrange("p b t h o -> p (b t) (h o)"), 1.0).then_inc(const_dve, 1)

            def bias_parts():
                for h in range(H):
                    dve.wait_ge(const_act, 8 + h)
                    nc.vector.tensor_copy(dist16[:, 0, h, :], dist[:, h, :]).then_inc(const_dve, 1)
                    dve.wait_ge(const_dve, 7 + 2 * h)
                    nc.vector.tensor_tensor(dist16[:, 1, h, :], dist[:, h, :], dist16[:, 0, h, :],
                                            ALU.subtract).then_inc(const_dve, 1)

            def prepare_experts():
                dve.wait_ge(c_moe, 176)
                nc.vector.tensor_scalar(w1raw[:, :, :], w1raw[:, :, :], WSCALE, None, ALU.mult)
                nc.vector.tensor_scalar(wr_raw[:, :], wr_raw[:, :], WSCALE, None, ALU.mult).then_inc(const_dve, 1)
                dve.wait_ge(const_dve, CONST_DVE + 1)
                nc.vector.tensor_copy(w1s[:, :, 0, :], w1raw[:, :, :])
                nc.vector.tensor_copy(wrs[:, 0, :], wr_raw[:, :])
                nc.vector.tensor_copy(b2hl[:, 0, :], b2raw[:, :]).then_inc(const_dve, 1)
                dve.wait_ge(const_dve, CONST_DVE + 2)
                nc.vector.tensor_tensor(w1s[:, :, 1, :], w1raw[:, :, :], w1s[:, :, 0, :], ALU.subtract)
                nc.vector.tensor_tensor(wrs[:, 1, :], wr_raw[:, :], wrs[:, 0, :], ALU.subtract)
                nc.vector.tensor_tensor(b2hl[:, 1, :], b2raw[:, :], b2hl[:, 0, :], ALU.subtract).then_inc(const_dve, 1)
                dve.wait_ge(const_dve, CONST_DVE + 3)
                nc.vector.tensor_scalar(b2rows[0:2, :], b2hl[:, 1, :], ident[0:2, 1:2], None, ALU.mult).then_inc(const_dve, 1)
                dve.wait_ge(const_dve, CONST_DVE + 4)
                nc.vector.scalar_tensor_tensor(b2rows[0:2, :], b2hl[:, 0, :], ident[0:2, 0:1], b2rows[0:2, :], ALU.mult,
                                               ALU.add).then_inc(const_dve, 1)

            def split_max(b, n):
                if not b.within(B):
                    return
                half, j = n // 4, n % 4
                dve.wait_ge(s1_ready, 8 * b.n + n + 1)
                nc.vector.tensor_reduce(stack[:, b.buf, half, 0, 2 * j:2 * j + 2, 24:25],
                                        s1[0:HALF, 512 * (n % 2):512 * (n % 2) + 2 * NSEL].rearrange("p (h m) -> p h m", h=2),
                                        AX.X, ALU.max, negate=True).then_inc(neg_max, 1)

            def step(t):
                squares = sq[:, :, :].rearrange("p t (g d) -> p (t g) d", d=D)
                scored, gated, turn, normed, last = t + 5, t + 4, t + 3, t + 2, t + (-1)
                if (t + 5).within(B):
                    b = t + 5
                    dve.wait_ge(x_loaded[b.buf], 16 * (b.turn + 1))
                    passed(dve, score, 2 * b.n)
                    nc.vector.tensor_tensor(prod[:, :, :], X[:, b.buf, :, 0:C],
                                            wscore[:, :].rearrange("p (o f) -> p o f", o=1).broadcast_to([TP, TC, C]),
                                            ALU.mult).then_inc(score, 1)
                if (t + 5).within(B):
                    b = t + 5
                    dve.wait_ge(score, 2 * b.n + 1)
                    passed(dve, gathered, b.n - 1)
                    nc.vector.tensor_reduce(X[:, b.buf, :, C:C + 1], prod[:, :, :], AX.X, ALU.add).then_inc(score, 1)
                if last.within(B):
                    dve.wait_ge(to_ready, last.n + 1)
                    to = MB[0:HALF, :].rearrange("p (g w) -> p g w", w=QW)
                    nc.vector.reciprocal(rz[:, :].rearrange("p (g o) -> p g o", o=1), to[:, :, D:D + 1]).then_inc(on_done, 1)
                    dve.wait_ge(on_done, 2 * last.n + 1)
                    nc.vector.tensor_tensor(on[:, :, :].rearrange("p t (g d) -> p (t g) d", d=D), to[:, :, 0:D],
                                            rz[:, :].rearrange("p (g o) -> p g o", o=1).broadcast_to([HALF, 16, D]),
                                            ALU.mult).then_inc(on_done, 1)
                if turn.within(B):
                    b = turn
                    dve.wait_ge(newton_done, 13 * b.n + 12)
                    passed(dve, xnT_ready, b.n)
                    for half in range(2):
                        nc.vector.tensor_scalar(xn[:, half, :], hsel[:, bass.ds(b.n, 1), half, :].rearrange("p o f -> p (o f)"),
                                                mv[:, b.buf, half, 0:1], ny[:, 4 * H + half:4 * H + half + 1], ALU.subtract,
                                                ALU.mult).then_inc(xn_done, 1)
                if normed.within(B):
                    b = normed
                    dve.wait_ge(newton_done, 13 * (b.n + 2))
                    passed(dve, stack_hi, 3 * b.n)
                    nc.vector.tensor_tensor(qn[:, :, :].rearrange("p t (g d) -> p t g d", d=D),
                                            qkv[:, b.buf, :, 0:2 * C].rearrange("p t (g d) -> p t g d", d=D),
                                            qk_factor[:, :].rearrange("p (t g o) -> p t g o", t=2, o=1).broadcast_to([HALF, 2, 2 * H, D]),
                                            ALU.mult).then_inc(stack_dve, 1)
                if gated.within(B):
                    b, k = gated, 7 * gated.n
                    dve.wait_ge(sel_out, 2 * (b.n + 1))
                    nc.vector.tensor_scalar(egate[:, :], egate[:, :], 1.0, None, ALU.add).then_inc(gate_steps, 1)
                    dve.wait_ge(gate_steps, k + 1)
                    nc.vector.reciprocal(gate[:, :], egate[:, :]).then_inc(gate_steps, 1)
                    dve.wait_ge(gate_steps, k + 2)
                    hb = hsel[:, bass.ds(b.n, 1), :, :].rearrange("p o t f -> p (o t) f")
                    nc.vector.tensor_tensor(hb, sel[:, :, 0:C],
                                            gate[:, :].rearrange("p (t o) -> p t o", o=1).broadcast_to([HALF, 2, C]),
                                            ALU.mult).then_inc(gate_steps, 1)
                if scored.within(B):
                    b = scored
                    dve.wait_ge(ranks_row, b.n + 1)
                    passed(dve, onehot_done, TC * (b.n - 1))
                    passed(dve, rank_done, TC * b.n)
                    for c in range(TC):
                        nc.vector.scalar_tensor_tensor(flags[:, c, :], MA[0:TP, 0:N], X[:, b.buf, c, C:C + 1],
                                                       before[:, c, :], ALU.subtract, ALU.is_gt,
                                                       accum_out=rank[:, b.buf, c:c + 1]).then_inc(rank_done, 1)
                split_max(t + 1, 0)
                if gated.within(B):
                    b, k = gated, 7 * gated.n
                    held(dve, gate_steps, k + 3, spare)
                    for half in range(2):
                        nc.vector.bn_stats(stats[:, half, :], hsel[:, bass.ds(b.n, 1), half, :].rearrange("p o f -> p (o f)")
                                           ).then_inc(gate_steps, 1)
                if last.within(B):
                    dve.wait_ge(pr_ready, last.n + 1)
                    hb = hsel[:, bass.ds(last.n, 1), :, :].rearrange("p o t f -> p (o t f)")
                    nc.vector.tensor_tensor(hb, hb, MB[0:HALF, 0:2 * C], ALU.add).then_inc(h_done, 1)
                split_max(t + 1, 1)
                if gated.within(B):
                    held(dve, gate_steps, k + 5, spare)
                    for half in range(2):
                        nc.vector.bn_aggr(mv[:, gated.buf, half, :], stats[:, half, :]).then_inc(gate_steps, 1)
                if (t + 4).within(B + 1):
                    b, p = t + 4, 5 * (t + 4).n
                    passed(dve, qkv_out, 2 * b.n)
                    passed(dve, newton_done, 13 * b.n)
                    nc.vector.tensor_reduce(nv[:, 0:4 * H].rearrange("p (g o) -> p g o", o=1), squares, AX.X,
                                            ALU.add).then_inc(norm_steps, 1)
                if (t + 4).within(B + 1):
                    b = t + 4
                    passed(dve, gate_steps, 7 * (b.n + 1) if b.within(B) else 7 * B)
                    nc.vector.tensor_scalar(nv[:, 4 * H:4 * H + 2], mv[:, b.buf, :, 1], EPS, None,
                                            ALU.add).then_inc(norm_steps, 1)
                split_max(t + 1, 2)
                if (t + 4).within(B + 1):
                    dve.wait_ge(norm_steps, p + 1)
                    nc.vector.tensor_scalar(nv[:, 0:4 * H], nv[:, 0:4 * H], 1e-24, None, ALU.max).then_inc(norm_steps, 1)
                if normed.within(B):
                    b = normed
                    dve.wait_ge(stack_hi, 3 * b.n + 1)
                    for qk, at in ((0, 2 * D), (1, D)):
                        nc.vector.tensor_tensor(stack[:, b.buf, :, qk, :, at:at + D],
                                                qn[:, :, qk * C:(qk + 1) * C].rearrange("p t (h d) -> p t h d", d=D),
                                                stack[:, b.buf, :, qk, :, 0:D], ALU.subtract).then_inc(stack_dve, 1)
                if (t + 4).within(B + 1):
                    dve.wait_ge(norm_steps, p + 3)
                    nc.vector.tensor_scalar(ni[:, :], nv[:, :].bitcast(i32), 1, None,
                                            ALU.logical_shift_right).then_inc(norm_steps, 1)
                split_max(t + 1, 3)
                if (t + 4).within(B + 1):
                    dve.wait_ge(norm_steps, p + 4)
                    nc.vector.tensor_scalar(ny[:, :].bitcast(i32), ni[:, :], -1.0, MAGIC, ALU.mult,
                                            ALU.add).then_inc(norm_steps, 1)
                split_max(t + 1, 4)
                split_max(t + 1, 5)
                split_max(t + 1, 6)
                split_max(t + 1, 7)


            def statistics(b):
                if isinstance(b.pair, int):
                    dve.wait_ge(h_done, CB * (b.n + 1))
                src = hsel[:, bass.ds(b.n * CB, CB), :, :].rearrange("p b t f -> p (b t) f")
                for j in range(CT):
                    nc.vector.bn_stats(n_stats[:, j, :], src[:, j, :]).then_inc(n_stat, 1)
                held(dve, n_stat, 19 * b.n + 8, spare)
                for j in range(CT):
                    nc.vector.bn_aggr(n_mv[:, j, :], n_stats[:, j, :]).then_inc(n_stat, 1)
                dve.wait_ge(n_stat, 19 * b.n + 16)
                nc.vector.tensor_scalar(n_v[:, :], n_mv[:, :, 1], 1.0 + EPS, EPS * EPS, ALU.mult, ALU.add).then_inc(n_stat, 1)

                dve.wait_ge(n_stat, 19 * b.n + 17)
                nc.vector.tensor_scalar(n_i[:, :], n_v[:, :].bitcast(i32), 1, None,
                                        ALU.logical_shift_right).then_inc(n_stat, 1)
                dve.wait_ge(n_stat, 19 * b.n + 18)
                nc.vector.tensor_scalar(n_y[:, :].bitcast(i32), n_i[:, :], -1.0, MAGIC, ALU.mult,
                                        ALU.add).then_inc(n_stat, 1)

            dve.wait_ge(c_wscore, 16)
            steps(dve, step, after=((-5, rest_of_setup), (-4, bias_parts), (B - 3, lambda: statistics(Batch(0, 0))), (B - 1, prepare_experts)))
            dve.wait_ge(h_done, B)

            def weight(c, j):
                if not c.within(NCH):
                    return
                if j == 0:
                    dve.wait_ge(gates, 16 * (c.n + 1))
                dve.wait_ge(y_ready, CT * c.n + j + 1)
                passed(dve, y_sum, CT * c.n + j - 1)
                nc.vector.tensor_tensor(yw[:, j % 2, :, :],
                                        s1[0:HALF, 512 * (j % 2):512 * (j % 2) + 512].rearrange("p (e d) -> p e d", e=E),
                                        wfull[:, c.buf, j, :].rearrange("p (e o) -> p e o", o=1).broadcast_to([HALF, E, C]),
                                        ALU.mult).then_inc(y_read, 1)

            def total(c, j):
                if not c.within(NCH):
                    return
                dve.wait_ge(y_read, CT * c.n + j + 1)
                if j == 0:
                    passed(dve, y_out, c.n - 1)
                nc.vector.tensor_reduce(yr[:, c.buf, j, :].rearrange("p (d o) -> p d o", o=1),
                                        yw[:, j % 2, :, :].rearrange("p e d -> p d e"), AX.X, ALU.add).then_inc(y_sum, 1)

            def b8(v):
                return v.rearrange("p (t o) -> p t o", o=1).broadcast_to([HALF, CT, E])

            def over_e(v):
                return v.rearrange("p (o e) -> p o e", o=1).broadcast_to([HALF, CT, E])

            def choose(b, i):
                if not b.within(NCH):
                    return
                k = 16 * b.n
                if i == 0:
                    dve.wait_ge(lg_ready, b.n + 1)
                    nc.vector.scalar_tensor_tensor(lg[:, :, :], MA[0:HALF, 0:CT * E].rearrange("p (t e) -> p t e", e=E),
                                                   1.0 / WSCALE, over_e(br_b[:, :]), ALU.mult, ALU.add).then_inc(gates, 1)
                    return
                dve.wait_ge(gates, k + i)
                src, top, oh = (lg, top1, oh1) if i < 7 else (lg2, top2, oh2)
                if i in (1, 7):
                    nc.vector.tensor_reduce(top[:, :].rearrange("p (t o) -> p t o", o=1), src[:, :, :], AX.X,
                                            ALU.max).then_inc(gates, 1)
                elif i in (2, 8):
                    nc.vector.tensor_tensor(eq[:, :, :], src[:, :, :], b8(top[:, :]), ALU.is_equal).then_inc(gates, 1)
                elif i in (3, 9):
                    nc.vector.tensor_tensor(eq[:, :, :], eq[:, :, :], over_e(prio[:, :]), ALU.mult).then_inc(gates, 1)
                elif i in (4, 10):
                    nc.vector.tensor_reduce(pick[:, :].rearrange("p (t o) -> p t o", o=1), eq[:, :, :], AX.X,
                                            ALU.max).then_inc(gates, 1)
                elif i in (5, 11):
                    nc.vector.tensor_tensor(oh[:, :, :], eq[:, :, :], b8(pick[:, :]), ALU.is_equal).then_inc(gates, 1)
                elif i == 6:
                    nc.vector.scalar_tensor_tensor(lg2[:, :, :], oh1[:, :, :], -1e30, lg[:, :, :], ALU.mult,
                                                   ALU.add).then_inc(gates, 1)
                elif i == 12:
                    nc.vector.tensor_tensor(dif[:, :], top1[:, :], top2[:, :], ALU.subtract).then_inc(gates, 1)
                elif i == 13:
                    dve.wait_ge(th_done, b.n + 1)
                    nc.vector.tensor_scalar(wa[:, :], th[:, :], 0.5, 0.5, ALU.mult, ALU.add)
                    nc.vector.tensor_scalar(wb[:, :], th[:, :], -0.5, 0.5, ALU.mult, ALU.add).then_inc(gates, 1)
                elif i == 14:
                    nc.vector.tensor_tensor(oh1[:, :, :], oh1[:, :, :], b8(wa[:, :]), ALU.mult)
                    nc.vector.tensor_tensor(oh2[:, :, :], oh2[:, :, :], b8(wb[:, :]), ALU.mult).then_inc(gates, 1)
                else:
                    nc.vector.tensor_tensor(wfull[:, b.buf, :, :], oh1[:, :, :], oh2[:, :, :], ALU.add).then_inc(gates, 1)

            def chunk(c):
                b = c + 2
                if b.within(NCH):
                    passed(dve, n_pool, 17 * b.n)
                    statistics(b)
                for j in range(CT):
                    weight(c, j)
                    choose(c + 1, 2 * j)
                    total(c, j)
                    choose(c + 1, 2 * j + 1)

            chunk_steps(dve, chunk)

        @block.tensor
        def _(pe):
            mm = nc.tensor.matmul
            def distances():
                for n in range(2 * H):
                    r = n // H
                    if n >= 4:
                        pe.wait_ge(const_act, 7 + n - 3)
                    mm(distance_bank(n), m2rep[:, n % H, :], hid[:, r * REL:(r + 1) * REL],
                       start=True, stop=True).then_inc(const_pe, 1)

            def hidden_layer():
                pe.wait_ge(c_rel, 16)
                pe.wait_ge(c_mlp, 64)
                for r in range(2):
                    mm(s1[0:META, 512 * r:512 * r + REL], m1t[:, :], rel[:, r * REL:(r + 1) * REL], start=True,
                       stop=True).then_inc(const_pe, 1)
                pe.wait_ge(const_pool, 5)
                pe.wait_ge(c_qkvw, 32)
                pe.wait_ge(c_projw, 16)
                for r in range(2):
                    nc.tensor.transpose(MB[0:C, r * META:(r + 1) * META], w_raw[:, r, :], ident[0:META, 0:META]).then_inc(const_pe, 1)
                nc.tensor.transpose(MB[0:C, 192:192 + C], wp_raw[:, :], ident[0:C, 0:C]).then_inc(const_pe, 1)
                pe.wait_ge(const_act, 5)
                pe.wait_ge(c_qkvb, 16)
                pe.wait_ge(c_projb, 16)
                pe.wait_ge(const_dve, 4)

            def row_max(b, n):
                if not b.within(B):
                    return
                half, j = n // 4, n % 4
                g, hh = j // 2, 2 * (j % 2)
                if n < 2:
                    pe.wait_ge(t1_out, 5 * b.n + 3 + 2 * n)
                if isinstance(b.pair, int) and b.n == 0 and n == 0:
                    pe.wait_ge(bias_loaded, 16 * 6)
                passed(pe, neg_max, 8 * b.n + n - 1)
                o = s1[0:HALF, 512 * (n % 2):512 * (n % 2) + 2 * NSEL]
                mm(o, ident16[:, 0:HALF], bias_q[:, half, 2 * j:2 * j + 2, :].rearrange("p h m -> p (h m)"),
                   start=True, stop=False)
                mm(o.rearrange("p (h m) -> p h m", h=2), qT1[:, b.buf, g, half * HALF:(half + 1) * HALF],
                   kT[:, b.buf, g, hh:hh + 2, 0:NSEL], start=False, stop=True).then_inc(s1_ready, 1)

            def logits(b, u):
                if not b.within(B):
                    return
                g, tile, k = u // 4, u // 2 % 2, u % 2
                rows = HALF - tile
                if u == 0:
                    pe.wait_ge(t2_out, b.n + 1)
                passed(pe, exp_done, 8 * b.n + u - 1)
                at, h0 = 512 * k, 4 * g + 2 * k
                for part in range(2):
                    mm(s2[0:rows, at:at + 2 * LQ], ident16[:, 0:rows],
                       bias_k[:, tile, part, h0:h0 + 2, :].rearrange("p h l -> p (h l)"),
                       start=part == 0, stop=part == 1)
                for j in range(2):
                    last = mm(s2[0:rows, at + j * LQ:at + (j + 1) * LQ],
                              kT[:, b.buf, g, 2 * k + j, tile * HALF:tile * HALF + rows], qT2[:, g, :],
                              start=False, stop=True, skip_group_check=True)
                last.then_inc(s2_ready, 1)

            def weigh(b, u):
                if not b.within(B):
                    return
                g, tile = u // 2, u % 2
                pe.wait_ge(exp_done, 8 * b.n + 2 * u + 2)
                if u == 0:
                    pe.wait_ge(v_done, 2 * (b.n + 1))
                    passed(pe, h_done, b.n)
                for hh in range(4):
                    last = mm(MB[32 * hh:32 * hh + QW, g * LQ:(g + 1) * LQ], V[:, b.buf, tile, 4 * g + hh, :],
                              P[:, u, hh, :], start=tile == 0, stop=tile == 1, tile_position=(0, 32 * hh),
                              skip_group_check=True)
                last.then_inc(pv_done, 1)

            def step(t):
                b = t + 4
                if b.within(B):
                    pe.wait_ge(onehot_done, TC * (b.n + 1))
                    for half in range(2):
                        for c in range(TC):
                            last = mm(MA[0:HALF, half * (C + 1):(half + 1) * (C + 1)],
                                      onehot[:, b.buf, c, half * HALF:(half + 1) * HALF], X[:, b.buf, c, :],
                                      start=c == 0, stop=c == TC - 1)
                    last.then_inc(gathered, 1)
                b = t
                if b.within(B):
                    pe.wait_ge(neg_max, 8 * (b.n + 1))
                    pe.wait_ge(t1_out, 5 * min(b.n + 2, B) if isinstance(b.pair, int) else 5 * (b.n + 2))
                    for g in range(2):
                        for half in range(2):
                            last = nc.tensor.transpose(t2_view[:, g, half * HALF:(half + 1) * HALF],
                                                       stack[:, b.buf, half, 0, 4 * g:4 * g + 4, :].rearrange("p h w -> p (h w)"),
                                                       ident16[0:HALF, 0:HALF])
                    last.then_inc(t2_ready, 1)
                b = t + (-1)
                if b.within(B):
                    pe.wait_ge(oT_out, b.n + 1)
                    for half in range(2):
                        for g in range(2):
                            last = nc.tensor.transpose(MB[0:HALF, (2 * half + g) * 128:(2 * half + g + 1) * 128],
                                                       oT[:, g, half * HALF:(half + 1) * HALF], ident[:, :])
                    last.then_inc(to_ready, 1)
                row_max(t + 1, 0)
                logits(t, 0)
                row_max(t + 1, 1)
                logits(t, 1)
                b = t + 3
                if b.within(B):
                    passed(pe, qkv_out, 2 * b.n)
                    held(pe, xn_done, 2 * (b.n + 1), spare)
                    for half in range(2):
                        last = nc.tensor.transpose(MC[0:C, half * HALF:(half + 1) * HALF], xn[:, half, :],
                                                   ident[0:HALF, 0:HALF])
                    last.then_inc(xnT_ready, 1)
                b = t + 5
                if b.within(B):
                    pe.wait_ge(score, 2 * (b.n + 1))
                    passed(pe, sel_out, 2 * b.n - 1)
                    for c in range(TC):
                        last = nc.tensor.transpose(MA[0:TP, c * TP:(c + 1) * TP],
                                                   X[:, b.buf, c, C:C + 1].broadcast_to([TP, TP]), ident[0:TP, 0:TP])
                    last.then_inc(ranks_row, 1)
                b = t + (-1)
                if b.within(B):
                    held(pe, on_done, 2 * (b.n + 1), spare)
                    for half in range(2):
                        last = nc.tensor.transpose(MB[0:C, half * HALF:(half + 1) * HALF], on[:, half, :],
                                                   ident[0:HALF, 0:HALF])
                    last.then_inc(onT_ready, 1)
                logits(t, 2)
                logits(t, 3)
                b = t + 3
                if b.within(B):
                    pe.wait_ge(xnT_out, b.n + 1)
                    for half in range(2):
                        last = mm(MC[0:HALF, half * 3 * C:(half + 1) * 3 * C], xnT[:, half * HALF:(half + 1) * HALF],
                                  w_qkv[:, :], start=True, stop=True)
                    last.then_inc(qkv_ready, 1)
                b = t + (-1)
                if b.within(B):
                    pe.wait_ge(onT_out, b.n + 1)
                    for half in range(2):
                        last = mm(MB[0:HALF, half * C:(half + 1) * C], onT[:, half * HALF:(half + 1) * HALF], w_proj[:, :],
                                  start=True, stop=True)
                    last.then_inc(pr_ready, 1)
                logits(t, 4)
                row_max(t + 1, 2)
                logits(t, 5)
                row_max(t + 1, 3)
                logits(t, 6)
                logits(t, 7)
                row_max(t + 1, 4)
                b = t + 2
                if b.within(B):
                    pe.wait_ge(stack_dve, 3 * (b.n + 1))
                    pe.wait_ge(stack_hi, 3 * (b.n + 1))
                    pe.wait_ge(max_clear, b.n + 1)
                    passed(pe, t2_out, b.n - 1)
                    for qk in range(2):
                        for g in range(2):
                            for half in range(2):
                                last = nc.tensor.transpose(t1_view[:, qk, g, half * HALF:(half + 1) * HALF],
                                                           stack[:, b.buf, half, qk, 4 * g:4 * g + 4, :].rearrange("p h w -> p (h w)"),
                                                           ident16[0:HALF, 0:HALF])
                    last.then_inc(t1_ready, 1)
                row_max(t + 1, 5)
                weigh(t, 0)
                weigh(t, 1)
                row_max(t + 1, 6)
                weigh(t, 2)
                row_max(t + 1, 7)
                weigh(t, 3)

            def transpose_normed(b):
                pe.wait_ge(n_pool, 17 * (b.n + 1))
                passed(pe, gates, 16 * (b.n - 1) + 1)
                for i in range(CT):
                    last = nc.tensor.transpose(MA16[:, i * HALF:(i + 1) * HALF], xs[:, i, :], ident16[0:HALF, 0:HALF])
                last.then_inc(xsT_ready, 1)

            def route(b):
                pe.wait_ge(xsT_out, b.n + 1)
                for i in range(CT):
                    for part in range(2):
                        last = mm(MA[0:HALF, i * E:(i + 1) * E], xsT[:, b.buf, i * HALF:(i + 1) * HALF],
                                  wrs[:, part, :], start=part == 0, stop=part == 1)
                last.then_inc(lg_ready, 1)

            pe.wait_ge(const_pool, 5)
            steps(pe, step, after=((-5, hidden_layer), (-4, distances)))

            transpose_normed(Batch(0, 0))
            pe.wait_ge(c_moe, 176)
            pe.wait_ge(h_done, B)
            nc.tensor.transpose(MB[:, 0:E], b1raw[:, :], ident[0:E, 0:E]).then_inc(const_pe, 1)
            pe.wait_ge(const_dve, CONST_DVE + 5)
            route(Batch(0, 0))

            def first(c, e):
                if not c.within(NCH):
                    return
                if e == 0:
                    pe.wait_ge(xsT_out, c.n + 1)
                passed(pe, gelu_done, E * c.n + e - 1)
                for k in range(2):
                    at = 1024 * (e % 2) + 512 * k
                    for part in range(2):
                        last = mm(s2[:, at:at + 376], w1s[:, e, part, :], xsT[:, c.buf, 376 * k:376 * (k + 1)],
                                  start=part == 0, stop=part == 1)
                last.then_inc(h_ready, 1)

            def second(c, j):
                if not c.within(NCH):
                    return
                if j == 0:
                    pe.wait_ge(gelu_done, E * (c.n + 1))
                passed(pe, y_read, CT * c.n + j - 1)
                o = s1[0:HALF, 512 * (j % 2):512 * (j % 2) + 512]
                mm(o, ones16[:, :], b2rows[:, :], start=True, stop=True)
                for e in range(E):
                    last = mm(o[:, e * C:(e + 1) * C], hT[:, c.buf, e, j * HALF:(j + 1) * HALF], w2[:, e, :],
                              start=False, stop=True, skip_group_check=True)
                last.then_inc(y_ready, 1)

            def chunk(c):
                b = c + 2
                for j in range(CT):
                    first(c + 1, j)
                    second(c, j)
                    if j == 6 and b.within(NCH):
                        transpose_normed(b)
                if b.within(NCH):
                    route(b)

            chunk_steps(pe, chunk)


LOG100 = 4.605170185988092
CONST_DVE = 6 + 2 * H
CONST_ACT = 7 + 2 * H

_INS = ["x", "L0_tok_score_proj", "L0_attn_qkv_w", "L0_attn_qkv_b", "L0_attn_proj_w", "L0_attn_proj_b",
        "L0_attn_logit_scale", "L0_attn_mlp1_w", "L0_attn_mlp1_b", "L0_attn_mlp2_w", "L0_attn_mlp2_b",
        "L0_ffn_gamma", "L0_ffn_beta", "L0_ffn_Wr", "L0_ffn_br", "L0_ffn_W1", "L0_ffn_b1", "L0_ffn_W2",
        "L0_ffn_b2"]


def kernel(**inputs):
    import numpy as np
    import concourse.bacc as bacc
    from concourse.bass_utils import run_bass_kernel_spmd

    d = np.arange(REL) - (NSEL - 1)
    r = (np.sign(d) * np.log1p(np.abs(d).astype(np.float32))).astype(np.float32)
    rel_log = np.stack([np.zeros(2 * REL, np.float32), np.concatenate([r, r[::-1]])])

    nc = bacc.Bacc("TRN2", target_bir_lowering=False, num_devices=1)
    arrays, args = {}, []
    for name in _INS:
        a = np.ascontiguousarray(inputs[name])
        arrays[f"in_{name}_dram"] = a
        args.append(nc.dram_tensor(f"in_{name}_dram", a.shape, mybir.dt.from_np(a.dtype), kind="ExternalInput").ap())
    arrays["rel_log_dram"] = rel_log
    args.append(nc.dram_tensor("rel_log_dram", rel_log.shape, mybir.dt.float32, kind="ExternalInput").ap())
    args.append(nc.dram_tensor("out_dram", (B, NSEL, C), mybir.dt.float32, kind="ExternalOutput").ap())
    audio_tower(nc, *args)
    result = run_bass_kernel_spmd(nc, [arrays], core_ids=[0])
    return result.results[0]["out_dram"]
```
